# Optimizing a Trainium2 kernel written in Bass

```python
import numpy as np
import jax
import jax.numpy as jnp

def _softmax(x, axis=-1):
    return jax.nn.softmax(x, axis=axis)

def _gelu(x):
    return jax.nn.gelu(x, approximate=True)

def _silu(x):
    return jax.nn.silu(x)

def _sigmoid(x):
    return jax.nn.sigmoid(x)

def _layernorm(x, axis=-1, eps=1e-05):
    m = jnp.mean(x, axis=axis, keepdims=True)
    v = jnp.var(x, axis=axis, keepdims=True)
    return (x - m) / jnp.sqrt(v + eps)

def _scatter_add(tgt, idx, src, axis=0):
    return tgt.at[idx].add(src)

def _segment_sum(src, seg, n):
    return jax.ops.segment_sum(src, seg, n)
kernel_name = 'mk_pixart_resid_d1_seqx_r8_a9efda'

def setup_inputs(seed: int=0):
    np.random.seed(seed)
    _w = jnp.asarray

    def _rec_inputs():
        import jax
        import jax.numpy as jnp
        _rk = jax.random.key(seed)
        x = -0.0005146 + 1 * jax.random.normal(jax.random.fold_in(_rk, 1), (1, 1024, 128), jnp.float32)
        _lenS = 1024 - jax.random.randint(jax.random.fold_in(_rk, 7), (1,), 0, max(1, 1024 // 4) + 1, jnp.int32)
        _lenS2 = 6404 - jax.random.randint(jax.random.fold_in(_rk, 8), (1,), 0, max(1, 6404 // 4) + 1, jnp.int32)
        _ctx_1024P = jax.random.normal(jax.random.fold_in(_rk, 11), (1, 16, 128), jnp.float32)
        _ctx_1024c = jax.random.dirichlet(jax.random.fold_in(_rk, 511), 0.3 * jnp.ones((16,), jnp.float32), (1, 6404))
        _ctx_1024t = jnp.einsum('bsk,bkd->bsd', _ctx_1024c, _ctx_1024P)
        _ctx_1024t = _ctx_1024t * jax.lax.rsqrt(jnp.mean(jnp.square(_ctx_1024t)) + 1e-12) * 0.953939
        ctx_1024 = -0.000125008 + 0.999885 * (_ctx_1024t + 0.3 * jax.random.normal(jax.random.fold_in(_rk, 611), (1, 6404, 128), jnp.float32))
        cond_1024 = -0.00920427 + 1.00102 * jax.random.normal(jax.random.fold_in(_rk, 12), (1, 128), jnp.float32)
        return (x, ctx_1024, cond_1024)
    x, ctx_1024, cond_1024 = _rec_inputs()

    def _L0_xcond_setup():
        import jax, jax.numpy as jnp
        import numpy as np
        DIM = 128
        DIM_HEAD = 64
        HEADS = 16
        INNER = DIM_HEAD * HEADS
        B, N1, N2 = (8, 512, 32)
        EPS = 1e-05

        def layer_norm(x, w, b):
            mu = jnp.mean(x, axis=-1, keepdims=True)
            var = jnp.var(x, axis=-1, keepdims=True)
            return (x - mu) * jax.lax.rsqrt(var + EPS) * w + b
        key = jax.random.key(seed)
        ks = jax.random.split(key, 10)
        return {'x': jax.random.normal(ks[0], (B, N1, DIM), jnp.float32), 'latents': jax.random.normal(ks[1], (B, N2, DIM), jnp.float32), 'shift': jax.random.normal(ks[2], (B, DIM), jnp.float32), 'scale': jax.random.normal(ks[3], (B, DIM), jnp.float32), 'ln1_w': jnp.ones((DIM,), jnp.float32), 'ln1_b': jnp.zeros((DIM,), jnp.float32), 'ln2_w': jnp.ones((DIM,), jnp.float32), 'ln2_b': jnp.zeros((DIM,), jnp.float32), 'Wq': jax.random.normal(ks[4], (INNER, DIM), jnp.float32) * 0.02, 'Wkv': jax.random.normal(ks[5], (2 * INNER, DIM), jnp.float32) * 0.02, 'Wo': jax.random.normal(ks[6], (DIM, INNER), jnp.float32) * 0.02}
    _L0_xcond_all = _L0_xcond_setup()
    _L0_xcond_in = {k: v for k, v in _L0_xcond_all.items() if k in ('ln1_w', 'ln1_b', 'ln2_w', 'ln2_b', 'Wq', 'Wkv', 'Wo')}
    del _L0_xcond_all

    def _L0_ffn_setup():
        import jax, jax.numpy as jnp
        import numpy as np
        EMBED_DIM = 128
        HIDDEN_DIM = 512
        NUM_EXPERTS = 8
        TOP_K = 2
        key = jax.random.key(seed)
        k_x, k_g, k_w1, k_w2 = jax.random.split(key, 4)
        x = jax.random.normal(k_x, (2, 64, EMBED_DIM), dtype=jnp.float32)
        gate_w = jax.random.normal(k_g, (NUM_EXPERTS, EMBED_DIM), dtype=jnp.float32) * (1.0 / np.sqrt(EMBED_DIM))
        w1 = jax.random.normal(k_w1, (NUM_EXPERTS, EMBED_DIM, HIDDEN_DIM), dtype=jnp.float32) * np.sqrt(2.0 / EMBED_DIM)
        b1 = jnp.zeros((NUM_EXPERTS, HIDDEN_DIM), dtype=jnp.float32)
        w2 = jax.random.normal(k_w2, (NUM_EXPERTS, HIDDEN_DIM, EMBED_DIM), dtype=jnp.float32) * np.sqrt(2.0 / HIDDEN_DIM)
        b2 = jnp.zeros((NUM_EXPERTS, EMBED_DIM), dtype=jnp.float32)
        return {'x': x, 'gate_w': gate_w, 'w1': w1, 'b1': b1, 'w2': w2, 'b2': b2}
    _L0_ffn_all = _L0_ffn_setup()
    _L0_ffn_in = {k: v for k, v in _L0_ffn_all.items() if k in ('gate_w', 'w1', 'b1', 'w2', 'b2')}
    del _L0_ffn_all
    return {'x': x, 'ctx_1024': ctx_1024, 'cond_1024': cond_1024, 'L0_xcond_ln1_w': _L0_xcond_in['ln1_w'], 'L0_xcond_ln1_b': _L0_xcond_in['ln1_b'], 'L0_xcond_ln2_w': _L0_xcond_in['ln2_w'], 'L0_xcond_ln2_b': _L0_xcond_in['ln2_b'], 'L0_xcond_Wq': _L0_xcond_in['Wq'], 'L0_xcond_Wkv': _L0_xcond_in['Wkv'], 'L0_xcond_Wo': _L0_xcond_in['Wo'], 'L0_ffn_gate_w': _L0_ffn_in['gate_w'], 'L0_ffn_w1': _L0_ffn_in['w1'], 'L0_ffn_b1': _L0_ffn_in['b1'], 'L0_ffn_w2': _L0_ffn_in['w2'], 'L0_ffn_b2': _L0_ffn_in['b2']}

def reference(x, ctx_1024, cond_1024, L0_xcond_ln1_w, L0_xcond_ln1_b, L0_xcond_ln2_w, L0_xcond_ln2_b, L0_xcond_Wq, L0_xcond_Wkv, L0_xcond_Wo, L0_ffn_gate_w, L0_ffn_w1, L0_ffn_b1, L0_ffn_w2, L0_ffn_b2):
    import jax
    import jax.numpy as jnp

    def _L0_xcond_ref(x, latents, shift, scale, ln1_w, ln1_b, ln2_w, ln2_b, Wq, Wkv, Wo):
        import jax, jax.numpy as jnp
        import numpy as np
        DIM = 128
        DIM_HEAD = 64
        HEADS = 16
        INNER = DIM_HEAD * HEADS
        B, N1, N2 = (8, 512, 32)
        EPS = 1e-05

        def layer_norm(x, w, b):
            mu = jnp.mean(x, axis=-1, keepdims=True)
            var = jnp.var(x, axis=-1, keepdims=True)
            return (x - mu) * jax.lax.rsqrt(var + EPS) * w + b
        x = layer_norm(x, ln1_w, ln1_b)
        lat = layer_norm(latents, ln2_w, ln2_b)
        lat = lat * (1.0 + scale[:, None, :]) + shift[:, None, :]
        b, n2, _ = lat.shape
        q = jnp.einsum('bld,ed->ble', lat, Wq)
        kv_in = jnp.concatenate((x, lat), axis=-2)
        kv = jnp.einsum('bld,ed->ble', kv_in, Wkv)
        k, v = jnp.split(kv, 2, axis=-1)

        def to_heads(t):
            bsz, L, _ = t.shape
            return t.reshape(bsz, L, HEADS, DIM_HEAD).transpose(0, 2, 1, 3)
        q, k, v = (to_heads(q), to_heads(k), to_heads(v))
        attn_scale = 1.0 / np.sqrt(np.sqrt(DIM_HEAD)).astype(np.float32)
        logits = jnp.einsum('bhqd,bhkd->bhqk', q * attn_scale, k * attn_scale)
        w = jax.nn.softmax(logits.astype(jnp.float32), axis=-1).astype(logits.dtype)
        out = jnp.einsum('bhqk,bhkd->bhqd', w, v)
        out = out.transpose(0, 2, 1, 3).reshape(b, n2, INNER)
        return jnp.einsum('ble,de->bld', out, Wo)

    def _L0_ffn_ref(x, gate_w, w1, b1, w2, b2):
        import jax, jax.numpy as jnp
        import numpy as np
        EMBED_DIM = 128
        HIDDEN_DIM = 512
        NUM_EXPERTS = 8
        TOP_K = 2
        orig_shape = x.shape
        xt = x.reshape(-1, EMBED_DIM)
        logits = xt @ gate_w.T
        probs = jax.nn.softmax(logits, axis=-1)
        top_w, top_i = jax.lax.top_k(probs, TOP_K)
        top_w = top_w / (top_w.sum(axis=-1, keepdims=True) + 1e-09)
        h = jnp.einsum('td,ndh->tnh', xt, w1) + b1
        h = jax.nn.gelu(h, approximate=False)
        out_all = jnp.einsum('tnh,nhd->tnd', h, w2) + b2
        sel = jnp.take_along_axis(out_all, top_i[:, :, None], axis=1)
        out = (sel * top_w[:, :, None]).sum(axis=1)
        return out.reshape(orig_shape)
    x = x + _L0_xcond_ref(ctx_1024, _layernorm(x, axis=-1), cond_1024, cond_1024, L0_xcond_ln1_w, L0_xcond_ln1_b, L0_xcond_ln2_w, L0_xcond_ln2_b, L0_xcond_Wq, L0_xcond_Wkv, L0_xcond_Wo)
    x = x + _L0_ffn_ref(_layernorm(x, axis=-1), L0_ffn_gate_w, L0_ffn_w1, L0_ffn_b1, L0_ffn_w2, L0_ffn_b2)
    return x

_drawn_inputs = setup_inputs


def setup_inputs(seed=0):
    import zlib

    import numpy as np

    out = dict(_drawn_inputs(seed))
    spreads = {'L0_xcond_ln1_w': (1.0, 0.2),
     'L0_xcond_ln1_b': (0.0, 0.1),
     'L0_xcond_ln2_w': (1.0, 0.6),
     'L0_xcond_ln2_b': (0.0, 0.1),
     'L0_ffn_b1': (0.0, 0.1),
     'L0_ffn_b2': (0.0, 0.1)}
    factors = {}
    for name, (base, spread) in spreads.items():
        noise = np.random.default_rng([zlib.crc32(name.encode()), seed]).standard_normal(out[name].shape)
        drawn = base * np.exp(spread * noise) if base else spread * noise
        out[name] = jnp.asarray(drawn.astype(out[name].dtype))
    for name, factor in factors.items():
        out[name] = (out[name] * factor).astype(out[name].dtype)
    return out
```

```python
from contextlib import ExitStack
import math

import concourse.bass as bass
from concourse import mybir

ALU = mybir.AluOpType
ACT = mybir.ActivationFunctionType
F32 = mybir.dt.float32
F16 = mybir.dt.float16
B16 = mybir.dt.bfloat16
I32 = mybir.dt.int32
AX_X = mybir.AxisListType.X
ds = bass.ds

P = 128
D = 128
DH = 64
HEADS = 16
PAIRS = HEADS // 2
NQ = 1024
QB = NQ // P
NCTX = 6404
CTXT = NCTX // P
ODD = NCTX - CTXT * P
NT = 1 + CTXT + QB
NKC = NT * P
LAT0 = (1 + CTXT) * P
VW = 2 * DH + 1
VS = VW + 1
LOOPS = (NT - 3) // 4
assert NT == 3 + 4 * LOOPS
EPS = 1e-5
WS = 16.0
EXP_SCALE = 1.0 / (math.sqrt(DH) * WS * WS)
SHIFT = 10 * math.log(2.0)
SUM_MIN, SUM_MAX = 128.0, 1e30
MROW = WS * WS * math.sqrt(DH)
PRE = 4 + 2 * (LOOPS + 1)
JOBS_A, JOBS_B = 8, 2 * (LOOPS + 1)
JOBS = JOBS_A + JOBS_B
ACT_A = 6
ACT_JOBS = ACT_A + JOBS_B
E, HID = 8, 512
HT = HID // P

MAXP = QB * (LOOPS + 1) + 2
MAXS = MAXP + 1
R_B1, R_GATE, R_LN1W, R_LN1B, R_LN2W, R_LN2B, R_COND, ROWS = 0, 32, 40, 41, 42, 43, 44, 45

CHUNKS = [(0, 12), (12, 12), (24, 12), (36, 12), (48, 3)]
GROUPS = [(4 * i, 4) for i in range(12)] + [(48, 3)]
NW = 8
NTR = NW + 2 + len(GROUPS)

SEMS = ["x_in", "w_in", "par_in", "ctx_in0", "ctx_in1", "ctx_in2", "ctx_in3", "ctx_in4", "ffnw_in",
        "par_t", "par_c", "tr_pe", "tr_act", "tr_dve", "dve_chain", "var_ready", "sqrt_ready", "norm_ready",
        "job_pe", "job_act", "job_dve", "scores_done", "exp_done", "rest_done", "pv_done", "o_copied",
        "on_ready", "wh_done", "wl_done", "max_pe", "max_dve", "total_ready", "good_sum",
        "flag_ready"]


def pixart_block(nc, x, ctx_in, cond, ln1w, ln1b, ln2w, ln2b, wq, wkv, wo, gate_w, w1, b1, w2, b2, out):
    with ExitStack() as stack:
        def sb(name, shape, dt):
            return stack.enter_context(nc.sbuf_tensor(name, shape, dt))

        def sem(name):
            return stack.enter_context(nc.semaphore(name))

        kvT = sb("kvT", [P, 2 * NKC], F16)
        K = sb("K", [P, 3 * NKC], F16)
        V = sb("V", [P, 3 * NT * VS], F16)
        Pf = sb("Pf", [P, 4 * NQ], F32)
        Pl = sb("Pl", [P, 4 * NQ], F16)
        Wk = sb("Wk", [P, 2, HEADS * DH], F16)
        Wv = sb("Wv", [P, 2, HEADS * DH], F16)
        Wq = sb("Wq", [P, 2, HEADS * P], F16)
        Q = sb("Q", [P, 2, 4 * NQ], F16)
        Oraw = sb("Oraw", [P, QB, VW], F32)
        On = sb("On", [P, QB, P], F32)
        OT = sb("OT", [P, 2, NQ], F16)
        Wo = sb("Wo", [P, 2, (PAIRS + 1) * P], F16)
        y = sb("y", [P, QB, P], F32)
        ident = sb("ident", [P, P], F32)
        ones = sb("ones", [P, P], F32)
        mask = sb("mask", [P, 1], F32)
        consts = sb("consts", [P, 2], F32)
        parT = sb("parT", [P, 48], F32)
        aff = sb("aff", [P, 2], F32)
        stats = sb("stats", [P, 12, 6], F32)
        mv = sb("mv", [P, 2, 12, 2], F32)
        rs = sb("rs", [P, 2, 12], F32)
        rt = sb("rt", [P, 12], F32)
        rden = sb("rden", [P, QB], F32)
        good = sb("good", [P, 3, QB], F32)
        flag = sb("flag", [1, 1], I32)
        mrow = sb("mrow", [1, NQ], F16)
        total = sb("total", [1, 1], F32)
        kconst = sb("kconst", [1, P], F16)
        b2s = sb("b2s", [E, P], F32)
        gates = sb("gates", [P, 9, QB, E], F32)
        small = sb("small", [P, 6, QB], F32)
        pri = sb("pri", [P, QB, E], F32)
        wT = sb("wT", [E, NQ], F32)
        psS = stack.enter_context(nc.psum_tensor("psS", [P, 4, 512], F32))
        psX = stack.enter_context(nc.psum_tensor("psX", [P, 4, 512], F32))
        psJ = psX[:, 3, :]

        kv_hi, kv_lo = kvT[:, 0:NKC], kvT[:, NKC:2 * NKC]
        A_SLOT = 1
        raw_ctx = K[:, NKC:3 * NKC].bitcast(F32)
        raw_w = Pf[:, :]
        raw_par = Pl[0:ROWS, 3072:3328].bitcast(F32)
        evac = Pl[:, 0:2048].bitcast(F32)
        lat0, lat1 = On, Oraw[:, :, 0:P]
        xt32 = On[:, :, :].rearrange("p b q -> p (b q)")
        xt16 = [OT[:, 0, :], OT[:, 1, :]]
        Pb = Pf[:, :].bitcast(B16)
        raw_w1 = K[:, 0:2 * E * HID].bitcast(F32)
        raw_w2 = V[:, 0:2 * E * HID].bitcast(F32)
        W1 = [kvT[:, 0:E * HID], kvT[:, E * HID:2 * E * HID]]
        W2 = [kvT[:, 2 * E * HID:3 * E * HID], V[:, 2 * E * HID:3 * E * HID]]

        def o_bank(b):
            return psX[:, b // 3, (b % 3) * VW:(b % 3) * VW + VW]

        runs = [{n: sem(f"{n}_{'first' if r == 0 else 'again'}") for n in SEMS} for r in range(2)]
        cst = sem("constants")
        mrow_max = sb("mrow_max", [P, QB * (LOOPS + 1)], F32)
        mq = sb("mq", [P, QB], F32)
        f = {n: sem("ffn_" + n) for n in ["chain", "var", "sqrt", "xt", "xt_t", "xt_c", "xt_split", "gate_pe", "shifted", "gexp",
                                          "gates", "wt_pe", "wt_c", "b2_pe", "h_pe", "gelu", "rest", "mix", "y_dve",
                                          "b2_in", "out"]}

        def slot_of(head, pair):
            return A_SLOT if head == 0 else (pair % 2) * 2

        def job0(pair):
            return PRE + JOBS * pair

        def act0(pair):
            return PRE + ACT_JOBS * pair

        def kcols(c):
            if isinstance(c, int) and c == 0:
                return 0, 3 * P
            return c * 512 - P, 512

        block = stack.enter_context(nc.Block())

        @block.sync
        def _(sp):
            def load(s):
                sp.dma_start(y[:], x.rearrange("o (p b) d -> p (o b) d", b=QB)).then_inc(s["x_in"], 16)
                small_rows = [(R_B1, b1.rearrange("e (j p) -> (e j) p", p=P)), (R_GATE, gate_w),
                              (R_LN1W, ln1w.rearrange("(a n) -> a n", a=1)), (R_LN1B, ln1b.rearrange("(a n) -> a n", a=1)),
                              (R_LN2W, ln2w.rearrange("(a n) -> a n", a=1)), (R_LN2B, ln2b.rearrange("(a n) -> a n", a=1)),
                              (R_COND, cond)]
                for row, src in small_rows:
                    sp.dma_start(raw_par[row:row + src.shape[0], :], src).then_inc(s["par_in"], 16)
                sp.dma_start(raw_w[:, 1024:3072].rearrange("p (i d) -> p i d", d=D),
                             wkv.rearrange("(i p) d -> p i d", p=P)).then_inc(s["w_in"], 16)
                sp.dma_start(raw_w[:, 0:1024].rearrange("p (i d) -> p i d", d=D),
                             wq.rearrange("(i p) d -> p i d", p=P)).then_inc(s["w_in"], 16)
                sp.dma_start(raw_w[:, 3072:4096], wo).then_inc(s["w_in"], 16)
                rows = ctx_in[0, 0:CTXT * P, :].rearrange("(p i) d -> p (i d)", i=CTXT)
                for c, (t0, n) in enumerate(CHUNKS):
                    if t0 == 0:
                        sp.dma_start(raw_ctx[:, 0:D], ctx_in[0, NCTX - P:NCTX, :]).then_inc(s["ctx_in0"], 16)
                    a = max(t0, 1)
                    sp.dma_start(raw_ctx[:, a * D:(t0 + n) * D],
                                 rows[:, (a - 1) * D:(t0 + n - 1) * D]).then_inc(s[f"ctx_in{c}"], 16)

            def load_experts(s):
                sp.wait_ge(s["pv_done"], HEADS - 1)
                sp.dma_start(raw_w1.rearrange("p (e h) -> p e h", e=E), w1.rearrange("e d h -> d e h")).then_inc(s["ffnw_in"], 16)
                sp.dma_start(raw_w2.rearrange("p (i d) -> p i d", d=D),
                             w2.rearrange("e (j p) d -> p (e j) d", p=P)).then_inc(s["ffnw_in"], 16)

            sp.dma_start(b2s[:], b2).then_inc(f["b2_in"], 16)
            load(runs[0])
            load_experts(runs[0])
            sp.wait_ge(runs[0]["flag_ready"], 1)
            again = sp.value_load(flag[0:1, 0:1], min_val=0, max_val=1)
            with sp.If(again > 0):
                load(runs[1])
                load_experts(runs[1])
                sp.nop()
            sp.wait_ge(f["y_dve"], E + 1)
            sp.dma_start(out.rearrange("o (p b) d -> p (o b) d", b=QB), y[:]).then_inc(f["out"], 16)
            sp.wait_ge(f["out"], 16)

        @block.gpsimd
        def _(pool):
            pool.memset(ident[:], 0.0).then_inc(cst, 1)
            pool.memset(ones[:], 1.0).then_inc(cst, 1)
            pool.memset(mask[:], 1.0).then_inc(cst, 1)
            pool.wait_ge(cst, 3)
            pool.affine_select(out=ident[:], in_=ident[:], compare_op=ALU.not_equal, fill=1.0, base=0,
                               pattern=[[-1, P]], channel_multiplier=1).then_inc(cst, 1)
            pool.memset(mask[0:P - ODD, :], 0.0).then_inc(cst, 1)
            pool.memset(consts[:, 0:1], EPS).then_inc(cst, 1)
            pool.memset(consts[:, 1:2], SHIFT).then_inc(cst, 1)
            pool.memset(kconst[:], MROW).then_inc(cst, 1)
            pool.memset(Wo[:, 0, 0:P], 0.0).then_inc(cst, 1)
            pool.memset(Wo[:, 1, 0:P], 0.0).then_inc(cst, 1)
            for e in range(E):
                pool.memset(pri[:, :, e:e + 1], float(E - e)).then_inc(cst, 1)
        N_CST = 10 + E

        @block.tensor
        def _(pe):
            def three(out_, wh, wl, xh, xl):
                pe.matmul(out_, wh, xh, start=True, stop=False)
                pe.matmul(out_, wh, xl, start=False, stop=False)
                return pe.matmul(out_, wl, xh, start=False, stop=True)

            def attention(s, exact):
                pe.wait_ge(cst, N_CST)
                pe.wait_ge(s["par_in"], 7 * 16)
                pe.transpose(psJ[:, 0:ROWS], raw_par[:, :], ident[0:ROWS, 0:ROWS]).then_inc(s["par_t"], 1)
                pe.wait_ge(s["w_in"], 3 * 16)

                def transposes(n, src, count):
                    if n >= 4:
                        pe.wait_ge(s["tr_dve"], n - 3)
                    for i in range(count):
                        last = pe.transpose(psS[:, n % 4, i * P:(i + 1) * P], src(i), ident[:])
                    last.then_inc(s["tr_pe"], 1)

                for n in range(NW):
                    transposes(n, lambda i: raw_w[:, (4 * n + i) * P:(4 * n + i + 1) * P], 4)
                pe.wait_ge(s["norm_ready"], 1)
                for n in range(2):
                    transposes(NW + n, lambda i: lat1[:, 4 * n + i, :], 4)
                for n, (t0, count) in enumerate(GROUPS):
                    if t0 % 12 == 0:
                        pe.wait_ge(s["norm_ready"], 2 + t0 // 12)
                    transposes(NW + 2 + n, lambda i: raw_ctx[:, (t0 + i) * D:(t0 + i + 1) * D], count)
                pe.wait_ge(s["tr_dve"], NTR)

                def q_job(bank, pair, head, half):
                    w = (pair * 2 + head) * P
                    xs = LAT0 + half * 512
                    return three(bank, Wq[:, 0, ds(w, P)], Wq[:, 1, ds(w, P)], kv_hi[:, xs:xs + 512], kv_lo[:, xs:xs + 512])

                def k_job(bank, pair, c):
                    c0, n = kcols(c)
                    return three(bank[:, 0:n], Wk[:, 0, ds(pair * P, P)], Wk[:, 1, ds(pair * P, P)],
                                 kv_hi[:, ds(c0, n)], kv_lo[:, ds(c0, n)])

                def v_tile(bank, pair, c, i):
                    c0, _ = kcols(c)
                    return three(bank[:, i * P:(i + 1) * P], kv_hi[:, ds(c0 + i * P, P)], kv_lo[:, ds(c0 + i * P, P)],
                                 Wv[:, 0, ds(pair * P, P)], Wv[:, 1, ds(pair * P, P)])

                def v_job(bank, pair, c):
                    for i in range(kcols(c)[1] // P):
                        last = v_tile(bank, pair, c, i)
                    return last

                for i in range(4):
                    q_job(psS[:, i, :], 0, i // 2, i % 2).then_inc(s["job_pe"], 1)
                pe.wait_ge(s["job_dve"], 1)
                k_job(psS[:, 0, :], 0, 0).then_inc(s["job_pe"], 1)
                pe.wait_ge(s["job_dve"], 2)
                v_job(psS[:, 1, :], 0, 0).then_inc(s["job_pe"], 1)
                with pe.Fori(0, LOOPS // 2) as g:
                    for u in range(2):
                        for kind, fn in enumerate((k_job, v_job)):
                            pe.wait_ge(s["job_dve"], g * 4 + (3 + 2 * u + kind))
                            fn(psS[:, (2 + 2 * u + kind) % 4, :], 0, g * 2 + (u + 1)).then_inc(s["job_pe"], 1)
                pe.wait_ge(s["job_dve"], PRE)

                def row_max(pair, head, jobs):
                    h = pair * 2 + head
                    slot = slot_of(head, pair) * NKC
                    qo = (pair % 2) * 2 * NQ + head * NQ
                    with pe.Fori(0, QB) as b:
                        pe.wait_ge(s["job_dve"], jobs)
                        def part(n, c0, width):
                            pe.wait_ge(s["max_dve"], n + 1)
                            pe.matmul(psJ[:, 0:width], Q[:, 0, ds(qo + b * P, P)], K[:, ds(c0 + slot, width)],
                                      start=True, stop=True).then_inc(s["max_pe"], 1)
                        n0 = h * MAXS + b * (LOOPS + 1)
                        part(n0, 0, 3 * P)
                        with pe.Fori(0, LOOPS) as g:
                            part(n0 + g + 1, g * 512 + 3 * P, 512)
                    n1 = h * MAXS + QB * (LOOPS + 1)
                    for half in range(2):
                        pe.wait_ge(s["max_dve"], n1 + 2 + half)
                        for i in range(4):
                            b = 4 * half + i
                            last = pe.matmul(psJ[0:1, i * P:(i + 1) * P], mq[:, b:b + 1], ident[:], start=True, stop=True)
                        last.then_inc(s["max_pe"], 1)
                    pe.wait_ge(s["max_dve"], n1 + 4)

                def scores(pair, head, t, par, v_step=None):
                    def v_tiles(which):
                        if v_step:
                            for i in which:
                                last = v_tile(psJ, *v_step[1:], i)
                            if 3 in which:
                                last.then_inc(s["job_pe"], 1)
                    n = pair * 2 * NT + head * NT + t
                    slot = slot_of(head, pair) * NKC
                    if v_step:
                        pe.wait_ge(s["job_dve"], v_step[0])
                    if not isinstance(n, int) or n >= 2:
                        pe.wait_ge(s["exp_done"], n - 1)
                    qo = (pair % 2) * 2 * NQ + head * NQ
                    k = K[:, ds(slot + t * P, P)]
                    for half in range(2):
                        bank = psS[:, 2 * par + half, :]
                        pe.matmul(bank, k, Q[:, 0, ds(qo + half * 512, 512)], start=True, stop=False)
                        v_tiles([0] if half == 0 else [2, 3])
                        last = pe.matmul(bank, k, Q[:, 1, ds(qo + half * 512, 512)], start=False, stop=not exact)
                        if exact:
                            last = pe.matmul(bank, kconst[:], mrow[:, half * 512:half * 512 + 512], start=False, stop=True)
                        if half == 0:
                            v_tiles([1])
                    last.then_inc(s["scores_done"], 1)

                def values(pair, head, t, buf, first=False, last_tile=False):
                    n = pair * 2 * NT + head * NT + t
                    pe.wait_ge(s["rest_done"], n + 1)
                    if first:
                        pe.wait_ge(s["o_copied"], pair * 2 + head + 1)
                    v0 = slot_of(head, pair) * NT * VS + t * VS
                    for b in range(QB):
                        hi = Pb[:, 2 * (buf * NQ + b * P) + 1:2 * (buf * NQ + (b + 1) * P):2]
                        lo = Pl[:, buf * NQ + b * P:buf * NQ + (b + 1) * P]
                        o = o_bank(b)
                        pe.matmul(o, hi, V[:, ds(v0, VW)], start=first and b % 3 == 0, stop=False, skip_group_check=True)
                        last = pe.matmul(o[:, 0:DH + 1], lo, V[:, ds(v0, DH + 1)], start=False, stop=last_tile,
                                         skip_group_check=True)
                    if last_tile:
                        last.then_inc(s["pv_done"], 1)

                def job(n, fn, *args):
                    pe.wait_ge(s["job_dve"], n)
                    fn(psJ, *args).then_inc(s["job_pe"], 1)

                def t_job(bank, pair, half):
                    pe.wait_ge(s["on_ready"], pair * 2 + 1)
                    for i in range(4):
                        last = pe.transpose(bank[:, i * P:(i + 1) * P],
                                            On[:, :, :].rearrange("p b q -> p (b q)")[:, ds(half * 512 + i * P, P)], ident[:])
                    return last

                def y_job(bank, pair, half):
                    for i in range(4):
                        q = half * 512 + i * P
                        last = three(bank[:, i * P:(i + 1) * P], OT[:, 0, ds(q, P)], OT[:, 1, ds(q, P)],
                                     Wo[:, 0, ds(pair * P, P)], Wo[:, 1, ds(pair * P, P)])
                    return last

                def group(pair, head, g, jobs=(), v_step=None):
                    for j in range(4):
                        for at, n, fn, args in jobs:
                            if at == j:
                                job(n, fn, *args)
                        scores(pair, head, g * 4 + (3 + j), (head + 3 + j) % 2, v_step if j == 2 else None)
                        values(pair, head, g * 4 + (1 + j), (1 + j) % 4)

                def body(pair, head, last_pair):
                    base = job0(pair)
                    scores(pair, head, 2, head)
                    if head == 1 and not last_pair:
                        job(base + JOBS_A + 1, v_job, pair + 1, 0)
                    values(pair, head, 0, 0, first=True)
                    if head == 0:
                        for u in range(2):
                            group(pair, 0, u * 2, [(1, base + u * 2, t_job, (pair, u))])
                            group(pair, 0, u * 2 + 1, [(1, base + u * 2 + 1, y_job, (pair, u))])
                        if not last_pair:
                            with pe.Fori(0, 2) as u:
                                for half in range(2):
                                    group(pair, 0, u * 2 + (4 + half), [(1, base + u * 2 + (4 + half), q_job, (pair + 1, u, half))])
                        with pe.Fori(4 if last_pair else 8, LOOPS) as g:
                            group(pair, 0, g)
                    else:
                        with pe.Fori(0, LOOPS) as g:
                            n = base + JOBS_A + 2 + g * 2
                            if last_pair:
                                group(pair, 1, g)
                            else:
                                group(pair, 1, g, [(0, n, k_job, (pair + 1, g + 1))], (n + 1, pair + 1, g + 1))
                    nxt = (pair, 1) if head == 0 else (pair + 1, 0)
                    more = not (last_pair and head == 1)
                    for t in range(2):
                        if more:
                            if t == 0:
                                jobs = base + (JOBS_A if head == 0 else JOBS) if not last_pair else base + 4
                                if exact:
                                    row_max(*nxt, jobs)
                                elif head == 1:
                                    pe.wait_ge(s["job_dve"], jobs)
                            if t == 0 and head == 0 and not last_pair:
                                job(base + JOBS_A, k_job, pair + 1, 0)
                            scores(*nxt, t, (nxt[1] + t) % 2)
                        values(pair, head, NT - 2 + t, (NT - 2 + t) % 4, last_tile=t == 1)

                if exact:
                    row_max(0, 0, PRE)
                scores(0, 0, 0, 0)
                scores(0, 0, 1, 1)
                with pe.Fori(0, PAIRS - 1) as p:
                    body(p, 0, False)
                    body(p, 1, False)
                body(PAIRS - 1, 0, True)
                body(PAIRS - 1, 1, True)
                base = job0(PAIRS - 1) + 4
                pe.wait_ge(s["exp_done"], HEADS * NT)
                for u in range(2):
                    t_job(psS[:, u, :], PAIRS, u).then_inc(s["job_pe"], 1)
                pe.wait_ge(s["job_dve"], base)
                pe.matmul(psJ[0:1, 0:QB], ones[:, 0:1], good[:, 0, :], start=True, stop=True).then_inc(s["good_sum"], 1)
                for u in range(2):
                    pe.wait_ge(s["job_dve"], base + 1 + u)
                    y_job(psS[:, 2 + u, :], PAIRS, u).then_inc(s["job_pe"], 1)

            attention(runs[0], False)
            pe.wait_ge(runs[0]["flag_ready"], 1)
            again = pe.value_load(flag[0:1, 0:1], min_val=0, max_val=1)
            with pe.If(again > 0):
                attention(runs[1], True)
                pe.nop()

            pe.wait_ge(f["xt"], 1)
            for half in range(2):
                for i in range(4):
                    last = pe.transpose(psS[:, half, i * P:(i + 1) * P], lat1[:, 4 * half + i, :], ident[:])
                last.then_inc(f["xt_t"], 1)
            pe.wait_ge(f["xt_c"], 2)
            for b in range(QB):
                last = pe.matmul(psX[:, 3, b * E:(b + 1) * E], xt32[:, b * P:(b + 1) * P], parT[:, R_GATE:R_GATE + E],
                                 start=True, stop=True)
            last.then_inc(f["gate_pe"], 1)
            pe.wait_ge(f["xt_split"], 1)

            def hidden(n, e, j):
                if not isinstance(n, int) or n >= 2:
                    pe.wait_ge(f["gelu"], n - 1)
                c = e * HID + j * P
                for half in range(2):
                    xs = half * 512
                    last = three(psS[:, 2 * (j % 2) + half, :], W1[0][:, ds(c, P)], W1[1][:, ds(c, P)],
                                 xt16[0][:, xs:xs + 512], xt16[1][:, xs:xs + 512])
                last.then_inc(f["h_pe"], 1)

            def mix(n, e, j, par):
                pe.wait_ge(f["rest"], n + 1)
                c = e * HID + j * P
                for b in range(QB):
                    hi = Pb[:, 2 * (j * NQ + b * P) + 1:2 * (j * NQ + (b + 1) * P):2]
                    lo = Pl[:, j * NQ + b * P:j * NQ + (b + 1) * P]
                    o = psX[:, 2 * par + b // 4, (b % 4) * P:(b % 4 + 1) * P]
                    pe.matmul(o, hi, W2[0][:, ds(c, P)], start=j == 0 and b % 4 == 0, stop=False, skip_group_check=True)
                    pe.matmul(o, hi, W2[1][:, ds(c, P)], start=False, stop=False, skip_group_check=True)
                    last = pe.matmul(o, lo, W2[0][:, ds(c, P)], start=False, stop=j == HT - 1, skip_group_check=True)
                last.then_inc(f["mix"], 1)

            hidden(0, 0, 0)
            hidden(1, 0, 1)

            def gate_rows():
                pe.wait_ge(f["gates"], 1)
                for half in range(2):
                    for i in range(4):
                        last = pe.transpose(psX[0:E, 2 + half, i * P:(i + 1) * P], gates[:, 0, 4 * half + i, :], ident[:])
                last.then_inc(f["wt_pe"], 1)

            def offsets():
                pe.wait_ge(f["wt_c"], 2)
                pe.wait_ge(f["b2_in"], 16)
                for b in range(QB):
                    last = pe.matmul(psX[:, 2 + b // 4, (b % 4) * P:(b % 4 + 1) * P], wT[:, b * P:(b + 1) * P], b2s[:],
                                     start=True, stop=True)
                last.then_inc(f["b2_pe"], 1)

            def two_experts(e, last):
                for par in range(2):
                    for j in range(HT):
                        n = (e + par) * HT + j
                        if j == 0 and not (isinstance(e, int) and e + par == 0):
                            pe.wait_ge(f["y_dve"], e + par)
                        if not (last and par == 1 and j >= 2):
                            hidden(n + 2, e + par + (j >= 2), (j + 2) % HT)
                        mix(n, e + par, j, par)
                        if isinstance(e, int) and n == 1:
                            gate_rows()
                        if isinstance(e, int) and n == 2:
                            offsets()

            two_experts(0, False)
            with pe.Fori(1, E // 2 - 1) as i:
                two_experts(i * 2, False)
            two_experts(E - 2, True)

        @block.scalar
        def _(act):
            def attention(s, exact):
                act.wait_ge(cst, N_CST)
                act.wait_ge(s["par_t"], 1)
                act.activation(parT[:, 0:ROWS], psJ[:, 0:ROWS], ACT.Copy).then_inc(s["par_c"], 1)

                roots = [0]

                def root(i, n):
                    act.wait_ge(s["var_ready"], roots[0] + 1)
                    act.activation(rs[:, i, 0:n], mv[:, i, 0:n, 1], ACT.Sqrt, bias=consts[:, 0:1]).then_inc(s["sqrt_ready"], 1)
                    roots[0] += 1

                root(0, QB)
                root(1, QB)
                for n in range(NW):
                    act.wait_ge(s["tr_pe"], n + 1)
                    src = psS[:, n % 4, :]
                    if n < 2:
                        for twin in range(2):
                            dst = Wq[:, 0, n * 1024:(n + 1) * 1024].rearrange("p (h t d) -> p h t d", t=2, d=DH)[:, :, twin, :]
                            last = act.activation(dst, src.rearrange("p (h d) -> p h d", d=DH), ACT.Copy, scale=WS)
                    elif n < 4:
                        last = act.activation(Wk[:, 0, (n - 2) * 512:(n - 1) * 512], src, ACT.Copy, scale=WS)
                    elif n < 6:
                        last = act.activation(Wv[:, 0, (n - 4) * 512:(n - 3) * 512], src, ACT.Copy, scale=WS)
                    else:
                        last = act.activation(Wo[:, 0, P + (n - 6) * 512:P + (n - 5) * 512], src, ACT.Copy, scale=WS)
                    last.then_inc(s["tr_act"], 1)
                root(0, 12)

                def split_kv(n, c0, width, scale, offset):
                    act.wait_ge(s["tr_pe"], n + 1)
                    if n >= NW + 2:
                        act.wait_ge(s["tr_dve"], n - 1)
                    src = psS[:, n % 4, 0:width]
                    act.activation(kv_hi[:, c0:c0 + width], src, ACT.Identity, bias=offset, scale=scale)
                    act.activation(evac[:, (n % 2) * 512:(n % 2) * 512 + width], src, ACT.Identity, bias=offset,
                                   scale=scale).then_inc(s["tr_act"], 1)

                act.wait_ge(s["par_c"], 3)
                for n in range(2):
                    split_kv(NW + n, LAT0 + n * 512, 512, aff[:, 0:1], aff[:, 1:2])
                for c, (t0, n) in enumerate(CHUNKS):
                    if c + 1 < len(CHUNKS):
                        root((c + 1) % 2, CHUNKS[c + 1][1])
                    for g, (a, cnt) in enumerate(GROUPS):
                        if t0 <= a < t0 + n:
                            split_kv(NW + 2 + g, a * P, cnt * P, parT[:, R_LN1W:R_LN1W + 1], parT[:, R_LN1B:R_LN1B + 1])

                def q_part(bank, pair, head, half):
                    act.activation(Q[:, 0, ds((pair % 2) * 2 * NQ + head * NQ + half * 512, 512)], bank, ACT.Copy)\
                       .then_inc(s["job_act"], 1)

                def k_part(bank, pair, c):
                    c0, n = kcols(c)
                    act.activation(K[0:DH, ds(A_SLOT * NKC + c0, n)], bank[0:DH, 0:n], ACT.Copy)
                    act.activation(K[DH:P, ds(slot_of(1, pair) * NKC + c0, n)], bank[DH:P, 0:n], ACT.Copy)\
                       .then_inc(s["job_act"], 1)

                def v_part(bank, pair, c):
                    first = isinstance(c, int) and c == 0
                    t0, n = (0, 3) if first else (c * 4 - 1, 4)
                    src = bank.rearrange("p (t d) -> p t d", d=P)
                    for head in range(2):
                        v0 = slot_of(head, pair) * NT * VS
                        if first:
                            act.activation(V[:, ds(v0, DH)], src[:, 0, head * DH:head * DH + DH], ACT.Copy, scale=mask[:, 0:1])
                        a = 1 if first else 0
                        dst = V[:, ds(v0 + (t0 + a) * VS, (n - a) * VS)].rearrange("p (t w) -> p t w", w=VS)[:, :, 0:DH]
                        last = act.activation(dst, src[:, a:n, head * DH:head * DH + DH], ACT.Copy)
                    last.then_inc(s["job_act"], 1)

                def pre(n, fn, *args):
                    act.wait_ge(s["job_pe"], n + 1)
                    fn(*args)

                for i in range(4):
                    pre(i, q_part, psS[:, i, :], 0, i // 2, i % 2)
                pre(4, k_part, psS[:, 0, :], 0, 0)
                pre(5, v_part, psS[:, 1, :], 0, 0)
                with act.Fori(0, LOOPS // 2) as g:
                    for u in range(2):
                        for kind, fn in enumerate((k_part, v_part)):
                            pre(g * 4 + (6 + 2 * u + kind), fn, psS[:, (2 + 2 * u + kind) % 4, :], 0, g * 2 + (u + 1))

                def exp(pair, head, t, par, buf):
                    act.wait_ge(s["scores_done"], pair * 2 * NT + head * NT + t + 1)
                    act.activation(Pf[:, buf * NQ:(buf + 1) * NQ], psS[:, 2 * par:2 * par + 2, :].rearrange("p a n -> p (a n)"),
                                   ACT.Exp, bias=consts[:, 1:2], scale=EXP_SCALE).then_inc(s["exp_done"], 1)

                def job(n, fn, *args):
                    act.wait_ge(s["job_pe"], n + 1)
                    fn(psJ, *args)

                def t_part(bank, half):
                    act.activation(OT[:, 0, ds(half * 512, 512)], bank, ACT.Copy).then_inc(s["job_act"], 1)

                def group(pair, head, g, jobs=()):
                    for j in range(4):
                        for at, n, fn, args in jobs:
                            if at == j:
                                job(n, fn, *args)
                        exp(pair, head, g * 4 + (3 + j), (head + 3 + j) % 2, (3 + j) % 4)

                def copy_out(pair, head):
                    act.wait_ge(s["pv_done"], pair * 2 + head + 1)
                    act.wait_ge(s["on_ready"], pair * 2 + head + 1)
                    for b in range(3):
                        n = min(3, QB - 3 * b)
                        last = act.activation(Oraw[:, 3 * b:3 * b + n, :].rearrange("p b w -> p (b w)"), psX[:, b, 0:n * VW], ACT.Copy)
                    last.then_inc(s["o_copied"], 1)

                def body(pair, head, last_pair):
                    base = job0(pair)
                    exp(pair, head, 2, (head + 2) % 2, 2)
                    if head == 1 and not last_pair:
                        job(base + JOBS_A + 1, v_part, pair + 1, 0)
                    if head == 0:
                        for u in range(2):
                            group(pair, 0, u * 2, [(1, base + u * 2, t_part, (u,))])
                            group(pair, 0, u * 2 + 1)
                        if not last_pair:
                            with act.Fori(0, 2) as u:
                                for half in range(2):
                                    group(pair, 0, u * 2 + (4 + half), [(1, base + u * 2 + (4 + half), q_part, (pair + 1, u, half))])
                        with act.Fori(4 if last_pair else 8, LOOPS) as g:
                            group(pair, 0, g)
                    elif not last_pair:
                        with act.Fori(0, LOOPS) as g:
                            n = base + JOBS_A + 2 + g * 2
                            group(pair, 1, g, [(0, n, k_part, (pair + 1, g + 1)), (2, n + 1, v_part, (pair + 1, g + 1))])
                    else:
                        with act.Fori(0, 6) as g:
                            group(pair, 1, g)
                        act.wait_ge(s["ffnw_in"], 32)
                        for raw, w in ((raw_w1, W1), (raw_w2, W2)):
                            g0 = 6 if raw is raw_w1 else 10
                            with act.Fori(0, 4) as g:
                                group(pair, 1, g + g0)
                                act.activation(w[0][:, ds(g * NQ, NQ)], raw[:, ds(g * NQ, NQ)], ACT.Copy, scale=WS)\
                                   .then_inc(s["wh_done"], 1)
                    if not (last_pair and head == 1):
                        nxt = (pair, 1) if head == 0 else (pair + 1, 0)
                        if head == 0 and not last_pair:
                            job(base + JOBS_A, k_part, pair + 1, 0)
                        for t in range(2):
                            exp(*nxt, t, (nxt[1] + t) % 2, t)
                    copy_out(pair, head)

                exp(0, 0, 0, 0, 0)
                exp(0, 0, 1, 1, 1)
                with act.Fori(0, PAIRS - 1) as p:
                    body(p, 0, False)
                    body(p, 1, False)
                body(PAIRS - 1, 0, True)
                body(PAIRS - 1, 1, True)
                base = job0(PAIRS - 1) + 4
                for u in range(2):
                    act.wait_ge(s["job_pe"], base + u + 1)
                    t_part(psS[:, u, :], u)

            attention(runs[0], False)
            act.wait_ge(runs[0]["flag_ready"], 1)
            again = act.value_load(flag[0:1, 0:1], min_val=0, max_val=1)
            with act.If(again > 0):
                attention(runs[1], True)
                act.nop()

            act.wait_ge(f["var"], 1)
            act.activation(rs[:, 0, 0:QB], mv[:, 0, 0:QB, 1], ACT.Sqrt, bias=consts[:, 0:1]).then_inc(f["sqrt"], 1)
            for half in range(2):
                act.wait_ge(f["xt_t"], half + 1)
                act.activation(xt32[:, half * 512:half * 512 + 512], psS[:, half, :], ACT.Copy).then_inc(f["xt_c"], 1)
            act.wait_ge(f["shifted"], 1)
            act.activation(gates[:, 1, :, :], gates[:, 1, :, :], ACT.Exp).then_inc(f["gexp"], 1)

            def gelu(n, e, j):
                act.wait_ge(f["h_pe"], n + 1)
                if not isinstance(n, int) or n >= 4:
                    act.wait_ge(f["mix"], n - 3)
                act.activation(Pf[:, j * NQ:(j + 1) * NQ],
                               psS[:, 2 * (j % 2):2 * (j % 2) + 2, :].rearrange("p a n -> p (a n)"), ACT.Gelu,
                               bias=parT[:, ds(R_B1 + e * HT + j, 1)], scale=1.0 / WS).then_inc(f["gelu"], 1)

            for j in range(HT):
                gelu(j, 0, j)
            with act.Fori(1, E) as e:
                for j in range(HT):
                    gelu(e * HT + j, e, j)

        @block.vector
        def _(dve):
            def attention(s, exact):
                count = [0]

                def link(ins):
                    ins.then_inc(s["dve_chain"], 1)
                    count[0] += 1
                    dve.wait_ge(s["dve_chain"], count[0])

                roots = [0]

                def variances(i, src, n):
                    for k in range(n):
                        last = dve.bn_stats(stats[:, k, :], src(k))
                    link(last)
                    for k in range(n):
                        last = dve.bn_aggr(mv[:, i, k, :], stats[:, k, :])
                    last.then_inc(s["var_ready"], 1)

                def inv_std(i, n):
                    roots[0] += 1
                    dve.wait_ge(s["sqrt_ready"], roots[0])
                    newton(dve, link, rs[:, i, 0:n], rt[:, 0:n], mv[:, i, 0:n, 1])

                def normalise(i, n, src, dst):
                    for k in range(n):
                        last = dve.tensor_scalar(dst(k), src(k), mv[:, i, k, 0:1], rs[:, i, k:k + 1], ALU.subtract, ALU.mult)
                    return last

                dve.wait_ge(cst, N_CST)
                ones_col = V[:, :].rearrange("p (t w) -> p t w", w=VS)[:, :, DH:DH + 1]
                link(dve.memset(ones_col, 1.0))
                for slot in range(3):
                    dve.tensor_copy(ones_col[:, slot * NT, :], mask[:])
                dve.wait_ge(s["x_in"], 16)
                variances(0, lambda k: y[:, k, :], QB)
                inv_std(0, QB)
                link(normalise(0, QB, lambda k: y[:, k, :], lambda k: lat0[:, k, :]))
                variances(1, lambda k: lat0[:, k, :], QB)
                inv_std(1, QB)
                normalise(1, QB, lambda k: lat0[:, k, :], lambda k: lat1[:, k, :]).then_inc(s["norm_ready"], 1)
                dve.wait_ge(s["par_c"], 1)
                link(dve.tensor_scalar(rden[:, 0:1], parT[:, R_COND:R_COND + 1], 1.0, None, ALU.add))
                dve.tensor_tensor(aff[:, 0:1], parT[:, R_LN2W:R_LN2W + 1], rden[:, 0:1], ALU.mult).then_inc(s["par_c"], 1)
                dve.scalar_tensor_tensor(aff[:, 1:2], parT[:, R_LN2B:R_LN2B + 1], rden[:, 0:1], parT[:, R_COND:R_COND + 1],
                                         ALU.mult, ALU.add).then_inc(s["par_c"], 1)

                def ctx_var(c):
                    t0, n = CHUNKS[c]
                    dve.wait_ge(s[f"ctx_in{c}"], 32 if c == 0 else 16)
                    variances(c % 2, lambda k: raw_ctx[:, (t0 + k) * D:(t0 + k + 1) * D], n)

                def ctx_norm(c):
                    t0, n = CHUNKS[c]
                    inv_std(c % 2, n)
                    normalise(c % 2, n, lambda k: raw_ctx[:, (t0 + k) * D:(t0 + k + 1) * D],
                              lambda k: raw_ctx[:, (t0 + k) * D:(t0 + k + 1) * D]).then_inc(s["norm_ready"], 1)

                ctx_var(0)
                for n in range(NW):
                    dve.wait_ge(s["tr_act"], n + 1)
                    src = psS[:, n % 4, :]
                    if n < 2:
                        for twin in range(2):
                            hl = [Wq[:, i, n * 1024:(n + 1) * 1024].rearrange("p (h t d) -> p h t d", t=2, d=DH)[:, :, twin, :]
                                  for i in range(2)]
                            last = dve.scalar_tensor_tensor(hl[1], src.rearrange("p (h d) -> p h d", d=DH), WS, hl[0],
                                                            ALU.mult, ALU.subtract)
                    else:
                        w, o = ((Wk, 0), (Wv, 0), (Wo, P))[n // 2 - 1]
                        o += (n % 2) * 512
                        last = dve.scalar_tensor_tensor(w[:, 1, o:o + 512], src, WS, w[:, 0, o:o + 512], ALU.mult, ALU.subtract)
                    last.then_inc(s["tr_dve"], 1)
                ctx_norm(0)

                def low_kv(n, c0, width):
                    dve.wait_ge(s["tr_act"], n + 1)
                    dve.tensor_tensor(kv_lo[:, c0:c0 + width], evac[:, (n % 2) * 512:(n % 2) * 512 + width],
                                      kv_hi[:, c0:c0 + width], ALU.subtract).then_inc(s["tr_dve"], 1)

                for n in range(2):
                    low_kv(NW + n, LAT0 + n * 512, 512)
                for c, (t0, n) in enumerate(CHUNKS):
                    if c + 1 < len(CHUNKS):
                        ctx_var(c + 1)
                    for g, (a, cnt) in enumerate(GROUPS):
                        if t0 <= a < t0 + n:
                            low_kv(NW + 2 + g, a * P, cnt * P)
                    if c + 1 < len(CHUNKS):
                        ctx_norm(c + 1)
                dve.wait_ge(s["tr_pe"], NW + 2)
                dve.memset(On[:, :, :], 0.0).then_inc(s["on_ready"], 1)
                dve.memset(good[:, 0, :], 0.0).then_inc(s["o_copied"], 1)

                def q_part(bank, pair, head, half):
                    o = (pair % 2) * 2 * NQ + head * NQ + half * 512
                    dve.tensor_tensor(Q[:, 1, ds(o, 512)], bank, Q[:, 0, ds(o, 512)], ALU.subtract).then_inc(s["job_dve"], 1)

                def k_part(bank, pair, c):
                    c0, n = kcols(c)
                    a, b = ds(A_SLOT * NKC + c0, n), ds(slot_of(1, pair) * NKC + c0, n)
                    dve.tensor_tensor(K[DH:P, a], bank[0:DH, 0:n], K[0:DH, a], ALU.subtract)
                    dve.tensor_tensor(K[0:DH, b], bank[DH:P, 0:n], K[DH:P, b], ALU.subtract).then_inc(s["job_dve"], 1)

                def v_part(bank, pair, c):
                    first = isinstance(c, int) and c == 0
                    t0, n = (0, 3) if first else (c * 4 - 1, 4)
                    src = bank.rearrange("p (t d) -> p t d", d=P)
                    for head in range(2):
                        v0 = slot_of(head, pair) * NT * VS
                        if first:
                            dve.scalar_tensor_tensor(V[:, ds(v0 + DH + 1, DH)], src[:, 0, head * DH:head * DH + DH], mask[:, 0:1],
                                                     V[:, ds(v0, DH)], ALU.mult, ALU.subtract)
                        a = 1 if first else 0
                        v = V[:, ds(v0 + (t0 + a) * VS, (n - a) * VS)].rearrange("p (t w) -> p t w", w=VS)
                        last = dve.tensor_tensor(v[:, :, DH + 1:VW], src[:, a:n, head * DH:head * DH + DH], v[:, :, 0:DH],
                                                 ALU.subtract)
                    last.then_inc(s["job_dve"], 1)

                def pre(n, fn, *args):
                    dve.wait_ge(s["job_act"], n + 1)
                    fn(*args)

                for i in range(4):
                    pre(i, q_part, psS[:, i, :], 0, i // 2, i % 2)
                pre(4, k_part, psS[:, 0, :], 0, 0)
                pre(5, v_part, psS[:, 1, :], 0, 0)
                with dve.Fori(0, LOOPS // 2) as g:
                    for u in range(2):
                        for kind, fn in enumerate((k_part, v_part)):
                            pre(g * 4 + (6 + 2 * u + kind), fn, psS[:, (2 + 2 * u + kind) % 4, :], 0, g * 2 + (u + 1))

                def rest(pair, head, t, buf):
                    dve.wait_ge(s["exp_done"], pair * 2 * NT + head * NT + t + 1)
                    dve.tensor_tensor(Pl[:, buf * NQ:(buf + 1) * NQ], Pf[:, buf * NQ:(buf + 1) * NQ],
                                      Pb[:, 2 * buf * NQ + 1:2 * (buf + 1) * NQ:2], ALU.subtract).then_inc(s["rest_done"], 1)

                def row_max(pair, head):
                    h = pair * 2 + head
                    with dve.Fori(0, QB) as b:
                        def part(n, i, width):
                            dve.wait_ge(s["max_pe"], n + 1)
                            dve.tensor_reduce(mrow_max[:, ds(b * (LOOPS + 1) + i, 1)], psJ[:, 0:width], AX_X, ALU.max)\
                               .then_inc(s["max_dve"], 1)
                        n0 = h * MAXP + b * (LOOPS + 1)
                        part(n0, 0, 3 * P)
                        with dve.Fori(0, LOOPS) as g:
                            part(n0 + g + 1, g + 1, 512)
                    done = h * MAXS + QB * (LOOPS + 1) + 1
                    dve.wait_ge(s["max_dve"], done)
                    dve.tensor_reduce(mq[:, :], mrow_max[:, :].rearrange("p (b c) -> p b c", b=QB), AX_X, ALU.max)\
                       .then_inc(s["max_dve"], 1)
                    for half in range(2):
                        dve.wait_ge(s["max_pe"], h * MAXP + QB * (LOOPS + 1) + 1 + half)
                        dve.tensor_scalar(mrow[:, half * 512:half * 512 + 512], psJ[0:1, :], -1.0 / MROW, None, ALU.mult)\
                           .then_inc(s["max_dve"], 1)

                def job(n, needs_act, fn, *args):
                    if needs_act is None:
                        dve.wait_ge(s["job_pe"], n + 1)
                    else:
                        dve.wait_ge(s["job_act"], needs_act + 1)
                    fn(psJ, *args)

                def t_part(bank, half):
                    dve.tensor_tensor(OT[:, 1, ds(half * 512, 512)], bank, OT[:, 0, ds(half * 512, 512)], ALU.subtract)\
                       .then_inc(s["job_dve"], 1)

                def y_part(bank, half, n):
                    o = y[:, :, :].rearrange("p b d -> p (b d)")[:, ds(half * 512, 512)]
                    dve.wait_ge(s["job_dve"], n)
                    dve.scalar_tensor_tensor(o, bank, 1.0 / (WS * WS), o, ALU.mult, ALU.add).then_inc(s["job_dve"], 1)

                def group(pair, head, g, jobs=()):
                    for j in range(4):
                        for at, n, na, fn, args in jobs:
                            if at == j:
                                job(n, na, fn, *args)
                        rest(pair, head, g * 4 + (3 + j), (3 + j) % 4)

                LINKS = 5

                def combine(pair, head):
                    h = pair * 2 + head
                    n0 = h * LINKS + links0
                    dve.wait_ge(s["o_copied"], h + 2)
                    dve.wait_ge(s["dve_chain"], n0)
                    den = Oraw[:, :, DH]
                    dve.tensor_scalar(good[:, 1, :], den, SUM_MIN, None, ALU.is_ge).then_inc(s["dve_chain"], 1)
                    dve.reciprocal(rden[:, :], den).then_inc(s["dve_chain"], 1)
                    dve.tensor_tensor(Oraw[:, :, 0:DH], Oraw[:, :, 0:DH], Oraw[:, :, DH + 1:VW], ALU.add)\
                       .then_inc(s["dve_chain"], 1)
                    dve.wait_ge(s["dve_chain"], n0 + 1)
                    dve.scalar_tensor_tensor(good[:, 2, :], den, SUM_MAX, good[:, 1, :], ALU.is_le, ALU.mult)\
                       .then_inc(s["dve_chain"], 1)
                    dve.wait_ge(s["dve_chain"], n0 + 4)
                    dve.tensor_tensor(good[:, 0, :], good[:, 0, :], good[:, 2, :], ALU.add).then_inc(s["dve_chain"], 1)
                    dve.tensor_tensor(On[:, :, head * DH:head * DH + DH], Oraw[:, :, 0:DH],
                                      rden[:, :].unsqueeze(2).to_broadcast([P, QB, DH]), ALU.mult)\
                       .then_inc(s["on_ready"], 1)

                def body(pair, head, last_pair):
                    base, ab = job0(pair), act0(pair)
                    rest(pair, head, 2, 2)
                    if head == 1 and not last_pair:
                        job(None, ab + ACT_A + 1, v_part, pair + 1, 0)
                    if head == 0:
                        for u in range(2):
                            group(pair, 0, u * 2, [(1, None, ab + u, t_part, (u,))])
                            group(pair, 0, u * 2 + 1, [(1, base + u * 2 + 1, None, y_part, (u, base + u * 2 + 1))])
                        if not last_pair:
                            with dve.Fori(0, 2) as u:
                                for half in range(2):
                                    group(pair, 0, u * 2 + (4 + half), [(1, None, ab + u * 2 + (2 + half), q_part, (pair + 1, u, half))])
                        with dve.Fori(4 if last_pair else 8, LOOPS) as g:
                            group(pair, 0, g)
                    elif not last_pair:
                        with dve.Fori(0, LOOPS) as g:
                            n = ab + ACT_A + 2 + g * 2
                            group(pair, 1, g, [(0, None, n, k_part, (pair + 1, g + 1)), (2, None, n + 1, v_part, (pair + 1, g + 1))])
                    else:
                        with dve.Fori(0, 6) as g:
                            group(pair, 1, g)
                        for k, (raw, w) in enumerate(((raw_w1, W1), (raw_w2, W2))):
                            with dve.Fori(0, 4) as g:
                                group(pair, 1, g + (6 + 4 * k))
                                dve.wait_ge(s["wh_done"], g + (4 * k + 1))
                                dve.scalar_tensor_tensor(w[1][:, ds(g * NQ, NQ)], raw[:, ds(g * NQ, NQ)], WS,
                                                         w[0][:, ds(g * NQ, NQ)], ALU.mult, ALU.subtract).then_inc(s["wl_done"], 1)
                    if not (last_pair and head == 1):
                        nxt = (pair, 1) if head == 0 else (pair + 1, 0)
                        if exact:
                            row_max(*nxt)
                        if head == 0 and not last_pair:
                            job(None, ab + ACT_A, k_part, pair + 1, 0)
                        for t in range(2):
                            rest(*nxt, t, t)
                    combine(pair, head)

                links0 = count[0]
                if exact:
                    dve.memset(mq[:, :], 0.0).then_inc(s["max_dve"], 1)
                    row_max(0, 0)
                rest(0, 0, 0, 0)
                rest(0, 0, 1, 1)
                with dve.Fori(0, PAIRS - 1) as p:
                    body(p, 0, False)
                    body(p, 1, False)
                body(PAIRS - 1, 0, True)
                body(PAIRS - 1, 1, True)
                base, ab = job0(PAIRS - 1) + 4, act0(PAIRS - 1) + 2
                for u in range(2):
                    dve.wait_ge(s["job_act"], ab + u + 1)
                    t_part(psS[:, u, :], u)
                dve.wait_ge(s["good_sum"], 1)
                dve.tensor_reduce(total[:], psJ[0:1, 0:QB], AX_X, ALU.add).then_inc(s["total_ready"], 1)
                dve.wait_ge(s["total_ready"], 1)
                dve.tensor_scalar(flag[:], total[:], float(HEADS * NQ), None, ALU.is_lt).then_inc(s["flag_ready"], 1)
                for u in range(2):
                    dve.wait_ge(s["job_pe"], base + 3 + u)
                    y_part(psS[:, 2 + u, :], u, base + 2 + u)
                dve.wait_ge(s["job_dve"], base + 4)

            attention(runs[0], False)
            dve.wait_ge(runs[0]["flag_ready"], 1)
            again = dve.value_load(flag[0:1, 0:1], min_val=0, max_val=1)
            with dve.If(again > 0):
                attention(runs[1], True)
                dve.nop()

            count = [0]

            def link(ins):
                ins.then_inc(f["chain"], 1)
                count[0] += 1
                dve.wait_ge(f["chain"], count[0])

            for k in range(QB):
                last = dve.bn_stats(stats[:, k, :], y[:, k, :])
            link(last)
            for k in range(QB):
                last = dve.bn_aggr(mv[:, 0, k, :], stats[:, k, :])
            last.then_inc(f["var"], 1)
            dve.wait_ge(f["sqrt"], 1)
            newton(dve, link, rs[:, 0, 0:QB], rt[:, 0:QB], mv[:, 0, 0:QB, 1])
            for k in range(QB):
                last = dve.tensor_scalar(lat1[:, k, :], y[:, k, :], mv[:, 0, k, 0:1], rs[:, 0, k:k + 1], ALU.subtract, ALU.mult)
            last.then_inc(f["xt"], 1)
            dve.wait_ge(f["xt_c"], 2)
            link(dve.tensor_copy(xt16[0], xt32))
            dve.tensor_tensor(xt16[1], xt32, xt16[0], ALU.subtract).then_inc(f["xt_split"], 1)

            def g(i):
                return gates[:, i, :, :]

            def wide(a):
                return a.unsqueeze(2).to_broadcast([P, QB, E])

            def sm(i):
                return small[:, i, :]

            dve.wait_ge(f["gate_pe"], 1)
            logits = psX[:, 3, 0:QB * E].rearrange("p (b e) -> p b e", e=E)
            link(dve.tensor_reduce(sm(0), logits, AX_X, ALU.max))
            dve.tensor_tensor(g(1), logits, wide(sm(0)), ALU.subtract).then_inc(f["shifted"], 1)

            def rest(n, j):
                dve.wait_ge(f["gelu"], n + 1)
                dve.tensor_tensor(Pl[:, j * NQ:(j + 1) * NQ], Pf[:, j * NQ:(j + 1) * NQ],
                                  Pb[:, 2 * j * NQ + 1:2 * (j + 1) * NQ:2], ALU.subtract).then_inc(f["rest"], 1)

            rest(0, 0)
            rest(1, 1)
            dve.wait_ge(f["gexp"], 1)
            link(dve.tensor_reduce(sm(1), g(1), AX_X, ALU.add))
            link(dve.reciprocal(sm(2), sm(1)))
            link(dve.tensor_tensor(g(2), g(1), wide(sm(2)), ALU.mult))

            def first_largest(probs, largest, key_max, picked):
                link(dve.tensor_reduce(largest, probs, AX_X, ALU.max))
                link(dve.tensor_tensor(g(3), probs, wide(largest), ALU.is_equal))
                link(dve.tensor_tensor(g(4), g(3), pri[:], ALU.mult))
                link(dve.tensor_reduce(key_max, g(4), AX_X, ALU.max))
                link(dve.tensor_tensor(picked, g(4), wide(key_max), ALU.is_equal))

            first_largest(g(2), sm(3), sm(4), g(5))
            link(dve.scalar_tensor_tensor(g(6), g(5), -2.0, g(2), ALU.mult, ALU.add))
            first_largest(g(6), sm(5), sm(4), g(7))
            link(dve.tensor_tensor(sm(0), sm(3), sm(5), ALU.add))
            link(dve.tensor_scalar(sm(1), sm(0), 1e-9, None, ALU.add))
            link(dve.reciprocal(sm(2), sm(1)))
            link(dve.tensor_tensor(g(3), g(5), g(7), ALU.add))
            link(dve.tensor_tensor(g(4), g(3), g(2), ALU.mult))
            link(dve.tensor_tensor(g(0), g(4), wide(sm(2)), ALU.mult))
            dve.tensor_scalar(g(8), g(0), 1.0 / WS, None, ALU.mult).then_inc(f["gates"], 1)

            rest(2, 2)
            dve.wait_ge(f["wt_pe"], 1)
            for half in range(2):
                dve.tensor_copy(wT[:, half * 512:half * 512 + 512], psX[0:E, 2 + half, :]).then_inc(f["wt_c"], 1)
            rest(3, 3)
            dve.wait_ge(f["b2_pe"], 1)
            for half in range(2):
                yh = y[:, half * 4:half * 4 + 4, :].rearrange("p b d -> p (b d)")
                last = dve.tensor_tensor(yh, psX[:, 2 + half, :], yh, ALU.add)
            last.then_inc(f["y_dve"], 1)

            def add(e, par):
                dve.wait_ge(f["mix"], e * HT + HT)
                dve.wait_ge(f["y_dve"], e + 1)
                for b in range(QB):
                    last = dve.scalar_tensor_tensor(y[:, b, :], psX[:, 2 * par + b // 4, (b % 4) * P:(b % 4 + 1) * P],
                                                    gates[:, 8, b, ds(e, 1)], y[:, b, :], ALU.mult, ALU.add)
                last.then_inc(f["y_dve"], 1)

            for n in range(HT, HT + 1):
                rest(n, n % HT)
            add(0, 0)
            for n in range(HT + 1, 2 * HT + 1):
                rest(n, n % HT)
            add(1, 1)
            with dve.Fori(1, E // 2 - 1) as i:
                for par in range(2):
                    for j in range(HT):
                        rest(i * 2 * HT + (par * HT + j + 1), (j + 1) % HT)
                    add(i * 2 + par, par)
            for n in range((E - 2) * HT + 1, (E - 1) * HT + 1):
                rest(n, n % HT)
            add(E - 2, 0)
            for n in range((E - 1) * HT + 1, E * HT):
                rest(n, n % HT)
            add(E - 1, 1)


def newton(dve, link, root, tmp, var):
    link(dve.reciprocal(root, root))
    link(dve.tensor_tensor(tmp, root, root, ALU.mult))
    link(dve.scalar_tensor_tensor(tmp, var, EPS, tmp, ALU.add, ALU.mult))
    link(dve.tensor_scalar(tmp, tmp, -0.5, 1.5, ALU.mult, ALU.add))
    link(dve.tensor_tensor(root, root, tmp, ALU.mult))


_INS = ["x", "ctx_1024", "cond_1024", "L0_xcond_ln1_w", "L0_xcond_ln1_b", "L0_xcond_ln2_w", "L0_xcond_ln2_b",
        "L0_xcond_Wq", "L0_xcond_Wkv", "L0_xcond_Wo", "L0_ffn_gate_w", "L0_ffn_w1", "L0_ffn_b1", "L0_ffn_w2",
        "L0_ffn_b2"]
_OUTS = [((1, NQ, D), "float32")]


def kernel(**inputs):
    import numpy as _np
    import concourse.bacc as _bacc
    from concourse import mybir as _mybir
    from concourse.bass_utils import run_bass_kernel_spmd as _run

    nc = _bacc.Bacc("TRN2", target_bir_lowering=False, num_devices=1)
    arrays, args = {}, []
    for name in _INS:
        a = _np.ascontiguousarray(inputs[name])
        arrays[f"in_{name}_dram"] = a
        args.append(nc.dram_tensor(f"in_{name}_dram", a.shape, _mybir.dt.from_np(a.dtype), kind="ExternalInput").ap())
    for i, (shape, dtype) in enumerate(_OUTS):
        args.append(nc.dram_tensor(f"out_{i}_dram", shape, _mybir.dt.from_np(_np.dtype(dtype)), kind="ExternalOutput").ap())
    pixart_block(nc, *args)
    r = _run(nc, [arrays], core_ids=[0])
    return r.results[0]["out_0_dram"]
```

```python
from contextlib import ExitStack
import math

import concourse.bass as bass
from concourse import mybir

ALU = mybir.AluOpType
ACT = mybir.ActivationFunctionType
F32 = mybir.dt.float32
F16 = mybir.dt.float16
B16 = mybir.dt.bfloat16
I32 = mybir.dt.int32
AX_X = mybir.AxisListType.X
ds = bass.ds

P = 128
D = 128
DH = 64
HEADS = 16
PAIRS = HEADS // 2
NQ = 1024
QB = NQ // P
NCTX = 6404
CTXT = NCTX // P
ODD = NCTX - CTXT * P
NT = 1 + CTXT + QB
NKC = NT * P
LAT0 = P
VW = 2 * DH + 1
VS = VW + 1
LOOPS = (NT - 3) // 4
assert NT == 3 + 4 * LOOPS
EPS = 1e-5
WS = 16.0
EXP_SCALE = 1.0 / (math.sqrt(DH) * WS * WS)
SHIFT = 10 * math.log(2.0)
SUM_MIN, SUM_MAX = 128.0, 1e30
MROW = WS * WS * math.sqrt(DH)
PRE = 4 + 2 * (LOOPS + 1)
JOBS_A, JOBS_B = 8, 2 * (LOOPS + 1)
JOBS = JOBS_A + JOBS_B
ACT_A = 6
ACT_JOBS = ACT_A + JOBS_B
E, HID = 8, 512
HT = HID // P

MAXP = QB * (LOOPS + 1) + 2
MAXS = MAXP + 1
R_B1, R_GATE, R_LN1W, R_LN1B, R_LN2W, R_LN2B, R_COND, ROWS = 0, 32, 40, 41, 42, 43, 44, 45

NW = 8
FSTEPS = LOOPS + 1
FS_B = 8
RAW_B = 4 * FS_B - 9
CHUNKS = [(0, RAW_B), (RAW_B, 1 + CTXT - RAW_B)]
ST_X, ST_LAT, ST_CTX = 0, QB, 2 * QB
NST = ST_CTX + 1 + CTXT

SEMS = ["x_in", "wq_in", "wkv_in", "wo_in", "par_in", "ctx_in0", "ctx_in1", "ffnw_in",
        "par_t", "par_c", "tr_pe", "tr_act", "tr_low", "dve_chain", "var_ready", "sqrt_ready", "lat_ready",
        "rs_ready", "centred", "norm_ready", "kvt_pe", "kvt_act", "kvt_high", "kvt_low",
        "job_pe", "job_act", "job_dve", "scores_done", "exp_done", "rest_done", "pv_done", "o_copied",
        "on_ready", "wh_done", "wl_done", "max_pe", "max_dve", "total_ready", "good_sum",
        "flag_ready"]


def pixart_block(nc, x, ctx_in, cond, ln1w, ln1b, ln2w, ln2b, wq, wkv, wo, gate_w, w1, b1, w2, b2, out):
    with ExitStack() as stack:
        def sb(name, shape, dt):
            return stack.enter_context(nc.sbuf_tensor(name, shape, dt))

        def sem(name):
            return stack.enter_context(nc.semaphore(name))

        kvT = sb("kvT", [P, 2 * NKC], F16)
        K = sb("K", [P, 3 * NKC], F16)
        V = sb("V", [P, 3 * NT * VS], F16)
        Pf = sb("Pf", [P, 4 * NQ], F32)
        Pl = sb("Pl", [P, 4 * NQ], F16)
        Wk = sb("Wk", [P, 2, HEADS * DH], F16)
        Wv = sb("Wv", [P, 2, HEADS * DH], F16)
        Wq = sb("Wq", [P, 2, HEADS * P], F16)
        Q = sb("Q", [P, 2, 4 * NQ], F16)
        Oraw = sb("Oraw", [P, QB, VW], F32)
        On = sb("On", [P, QB, P], F32)
        OT = sb("OT", [P, 2, NQ], F16)
        Wo = sb("Wo", [P, 2, PAIRS * P], F16)
        y = sb("y", [P, QB, P], F32)
        ident = sb("ident", [P, P], F32)
        ones = sb("ones", [P, P], F32)
        mask = sb("mask", [P, 1], F32)
        consts = sb("consts", [P, 2], F32)
        parT = sb("parT", [P, 48], F32)
        aff = sb("aff", [P, 2], F32)
        stats = sb("stats", [P, NST, 6], F32)
        mv = sb("mv", [P, NST, 2], F32)
        rs = sb("rs", [P, NST], F32)
        rt = sb("rt", [P, NST], F32)
        rden = sb("rden", [P, QB], F32)
        good = sb("good", [P, 3, QB], F32)
        flag = sb("flag", [1, 1], I32)
        chunk_max = sb("chunk_max", [P, QB * (LOOPS + 1)], F32)
        mq = sb("mq", [P, QB], F32)
        mrow = sb("mrow", [1, NQ], F16)
        total = sb("total", [1, 1], F32)
        kconst = sb("kconst", [1, P], F16)
        b2s = sb("b2s", [E, P], F32)
        gate_hl = sb("gate_hl", [P, 2, E], F16)
        gates = sb("gates", [P, 9, QB, E], F32)
        small = sb("small", [P, 6, QB], F32)
        pri = sb("pri", [P, QB, E], F32)
        psS = stack.enter_context(nc.psum_tensor("psS", [P, 4, 512], F32))
        psX = stack.enter_context(nc.psum_tensor("psX", [P, 4, 512], F32))
        psJ = psX[:, 3, :]

        kv_hi, kv_lo = kvT[:, 0:NKC], kvT[:, NKC:2 * NKC]
        A_SLOT = 1
        raw_a = K[:, 2 * NKC:3 * NKC].bitcast(F32)
        raw_b = V[:, 2 * NT * VS:3 * NT * VS].bitcast(F32)
        evac_w = K[:, 0:8 * NQ].bitcast(F32)
        raw_w = Pf[:, :]
        raw_par = Pl[0:ROWS, 3072:3328].bitcast(F32)
        normed = On[:, :, :].rearrange("p b q -> p (b q)")
        evac = OT[:, :, :].rearrange("p a q -> p (a q)").bitcast(F32)
        lat0, lat1 = On, Oraw[:, :, 0:P]
        wT = Oraw[0:E, :, :].rearrange("p b w -> p (b w)")[:, 0:NQ]
        xt16 = [OT[:, 0, :], OT[:, 1, :]]
        Pb = Pf[:, :].bitcast(B16)
        raw_w1 = K[:, 0:2 * E * HID].bitcast(F32)
        raw_w2 = V[:, 0:2 * E * HID].bitcast(F32)
        W1 = [kvT[:, 0:E * HID], kvT[:, E * HID:2 * E * HID]]
        W2 = [kvT[:, 2 * E * HID:3 * E * HID], V[:, 2 * E * HID:3 * E * HID]]

        def o_bank(b):
            return psX[:, b // 3, (b % 3) * VW:(b % 3) * VW + VW]

        runs = [{n: sem(f"{n}_{'first' if r == 0 else 'again'}") for n in SEMS} for r in range(2)]
        cst = sem("constants")
        f = {n: sem("ffn_" + n) for n in ["chain", "var", "sqrt", "xt", "xt_t", "xt_c", "xt_split", "gw_high", "gate_pe", "shifted", "gexp",
                                          "gates", "wt_pe", "wt_c", "b2_pe", "h_pe", "gelu", "rest", "mix", "y_dve",
                                          "b2_in", "out"]}

        def slot_of(head, pair):
            return A_SLOT if head == 0 else (pair % 2) * 2

        def raw_tile(r, n=1):
            return raw_a[:, r * D:(r + n) * D] if r < RAW_B else raw_b[:, (r - RAW_B) * D:(r - RAW_B + n) * D]

        def job0(pair):
            return PRE - 4 + JOBS * pair

        def act0(pair):
            return PRE - 2 + ACT_JOBS * pair

        def kcols(c):
            if isinstance(c, int) and c == 0:
                return 0, 3 * P
            return c * 512 - P, 512

        def fcols(m):
            if isinstance(m, int) and m < 2:
                return [(LAT0 + m * 512, 0, 512)]
            if isinstance(m, int) and m == 2:
                return [(0, 0, P), ((1 + QB) * P, P, 2 * P)]
            return [(m * 512 - P, 0, 512)]

        block = stack.enter_context(nc.Block())

        @block.sync
        def _(sp):
            def load(s):
                sp.dma_start(y[:], x.rearrange("o (p b) d -> p (o b) d", b=QB)).then_inc(s["x_in"], 16)
                sp.dma_start(raw_w[:, 0:1024].rearrange("p (i d) -> p i d", d=D),
                             wq.rearrange("(i p) d -> p i d", p=P)).then_inc(s["wq_in"], 16)
                small_rows = [(R_B1, b1.rearrange("e (j p) -> (e j) p", p=P)), (R_GATE, gate_w),
                              (R_LN1W, ln1w.rearrange("(a n) -> a n", a=1)), (R_LN1B, ln1b.rearrange("(a n) -> a n", a=1)),
                              (R_LN2W, ln2w.rearrange("(a n) -> a n", a=1)), (R_LN2B, ln2b.rearrange("(a n) -> a n", a=1)),
                              (R_COND, cond)]
                for row, src in small_rows:
                    sp.dma_start(raw_par[row:row + src.shape[0], :], src).then_inc(s["par_in"], 16)
                sp.dma_start(raw_w[:, 1024:3072].rearrange("p (i d) -> p i d", d=D),
                             wkv.rearrange("(i p) d -> p i d", p=P)).then_inc(s["wkv_in"], 16)
                sp.dma_start(raw_w[:, 3072:4096], wo).then_inc(s["wo_in"], 16)
                rows = ctx_in[0, 0:CTXT * P, :].rearrange("(p i) d -> p (i d)", i=CTXT)
                sp.dma_start(raw_tile(0), ctx_in[0, NCTX - P:NCTX, :]).then_inc(s["ctx_in0"], 16)
                for c, (t0, n) in enumerate(CHUNKS):
                    a = max(t0, 1)
                    sp.dma_start(raw_tile(a, t0 + n - a), rows[:, (a - 1) * D:(t0 + n - 1) * D]).then_inc(s[f"ctx_in{c}"], 16)

            def load_experts(s):
                sp.wait_ge(s["pv_done"], HEADS - 1)
                sp.dma_start(raw_w1.rearrange("p (e h) -> p e h", e=E), w1.rearrange("e d h -> d e h")).then_inc(s["ffnw_in"], 16)
                sp.dma_start(raw_w2.rearrange("p (i d) -> p i d", d=D),
                             w2.rearrange("e (j p) d -> p (e j) d", p=P)).then_inc(s["ffnw_in"], 16)

            sp.dma_start(b2s[:], b2).then_inc(f["b2_in"], 16)
            load(runs[0])
            load_experts(runs[0])
            sp.wait_ge(runs[0]["flag_ready"], 1)
            again = sp.value_load(flag[0:1, 0:1], min_val=0, max_val=1)
            with sp.If(again > 0):
                sp.wait_ge(runs[0]["job_dve"], job0(PAIRS - 1) + 8)
                load(runs[1])
                load_experts(runs[1])
                sp.nop()
            sp.wait_ge(f["y_dve"], E + 1)
            sp.dma_start(out.rearrange("o (p b) d -> p (o b) d", b=QB), y[:]).then_inc(f["out"], 16)
            sp.wait_ge(f["out"], 16)

        @block.gpsimd
        def _(pool):
            pool.memset(ident[:], 0.0).then_inc(cst, 1)
            pool.memset(ones[:], 1.0).then_inc(cst, 1)
            pool.memset(mask[:], 1.0).then_inc(cst, 1)
            pool.wait_ge(cst, 3)
            pool.affine_select(out=ident[:], in_=ident[:], compare_op=ALU.not_equal, fill=1.0, base=0,
                               pattern=[[-1, P]], channel_multiplier=1).then_inc(cst, 1)
            pool.memset(mask[0:P - ODD, :], 0.0).then_inc(cst, 1)
            pool.memset(consts[:, 0:1], EPS).then_inc(cst, 1)
            pool.memset(consts[:, 1:2], SHIFT).then_inc(cst, 1)
            pool.memset(kconst[:], MROW).then_inc(cst, 1)
            for e in range(E):
                pool.memset(pri[:, :, e:e + 1], float(E - e)).then_inc(cst, 1)

            def ctx_tiles(s):
                def norm(m, par, second):
                    special = isinstance(m, int) and m == 2
                    n = 3 if special else 4
                    r = 0 if special else m * 4 - 9
                    src = raw_b[:, ds((m * 4 - (9 + RAW_B)) * D, n * D)] if second else raw_a[:, ds(r * D, n * D)]
                    src = src.rearrange("p (t d) -> p t d", d=D)
                    dst = normed[:, par * 512:par * 512 + n * D].rearrange("p (t d) -> p t d", d=D)
                    at = ds(r + ST_CTX, n)
                    if isinstance(m, int):
                        pool.wait_ge(s["rs_ready"], 1 + sum(r >= t0 for t0, _ in CHUNKS[1:]))
                    if not (isinstance(m, int) and m <= 3):
                        pool.wait_ge(s["kvt_pe"], m - 1)
                    pool.tensor_tensor(dst, src, mv[:, at, 0:1].to_broadcast([P, n, D]), ALU.subtract)\
                        .then_inc(s["centred"], 1)
                    pool.wait_ge(s["centred"], m - 1)
                    pool.tensor_tensor(dst, dst, rs[:, at].unsqueeze(2).to_broadcast([P, n, D]), ALU.mult)\
                        .then_inc(s["norm_ready"], 1)

                def low(m, par):
                    pool.wait_ge(s["kvt_act"], m + 1)
                    if not (isinstance(m, int) and m <= 2):
                        pool.tensor_copy(kv_hi[:, ds(m * 512 - P, 512)], evac[:, par * 512:par * 512 + 512])\
                            .then_inc(s["kvt_high"], 1)
                        pool.wait_ge(s["kvt_high"], m - 2)
                    for c0, o, n in fcols(m):
                        last = pool.tensor_tensor(kv_lo[:, ds(c0, n)], evac[:, par * 512 + o:par * 512 + o + n],
                                                  kv_hi[:, ds(c0, n)], ALU.subtract)
                    last.then_inc(s["kvt_low"], 1)

                for n in range(NW):
                    pool.wait_ge(s["tr_act"], n + 1)
                    src = evac_w[:, n * 512:(n + 1) * 512]
                    if n < 2:
                        hl = [Wq[:, i, n * 1024:(n + 1) * 1024].rearrange("p (h t d) -> p h t d", t=2, d=DH) for i in range(2)]
                        for twin in range(2):
                            last = pool.tensor_tensor(hl[1][:, :, twin, :], src.rearrange("p (h d) -> p h d", d=DH),
                                                      hl[0][:, :, twin, :], ALU.subtract)
                    else:
                        w, o = (Wk, Wv, Wo)[n // 2 - 1], (n % 2) * 512
                        last = pool.tensor_tensor(w[:, 1, o:o + 512], src, w[:, 0, o:o + 512], ALU.subtract)
                    last.then_inc(s["tr_low"], 1)
                norm(2, 0, False)
                norm(3, 1, False)
                low(2, 0)
                norm(4, 0, False)
                low(3, 1)
                norm(5, 1, False)
                low(4, 0)
                pool.wait_ge(s["rs_ready"], len(CHUNKS))
                with pool.Fori(3, FS_B // 2) as i:
                    for u in range(2):
                        norm(i * 2 + u, u, False)
                        low(i * 2 + (u - 1), 1 - u)
                with pool.Fori(FS_B // 2, (FSTEPS - 1) // 2) as i:
                    for u in range(2):
                        norm(i * 2 + u, u, True)
                        low(i * 2 + (u - 1), 1 - u)
                norm(FSTEPS - 1, 0, True)
                low(FSTEPS - 2, 1)
                low(FSTEPS - 1, 0)

            ctx_tiles(runs[0])
            pool.wait_ge(runs[0]["flag_ready"], 1)
            again = pool.value_load(flag[0:1, 0:1], min_val=0, max_val=1)
            with pool.If(again > 0):
                ctx_tiles(runs[1])
                pool.nop()
        N_CST = 8 + E

        @block.tensor
        def _(pe):
            def three(out_, wh, wl, xh, xl):
                pe.matmul(out_, wh, xh, start=True, stop=False)
                pe.matmul(out_, wh, xl, start=False, stop=False)
                return pe.matmul(out_, wl, xh, start=False, stop=True)

            def attention(s, exact):
                pe.wait_ge(cst, N_CST)
                pe.wait_ge(s["par_in"], 7 * 16)
                pe.transpose(psJ[:, 0:ROWS], raw_par[:, :], ident[0:ROWS, 0:ROWS]).then_inc(s["par_t"], 1)
                def transposes(n, src, count):
                    if n >= 4:
                        pe.wait_ge(s["tr_act"], n - 3)
                    for i in range(count):
                        last = pe.transpose(psS[:, n % 4, i * P:(i + 1) * P], src(i), ident[:])
                    last.then_inc(s["tr_pe"], 1)

                for n in range(NW):
                    arrived = {0: "wq_in", 2: "wkv_in", 6: "wo_in"}.get(n)
                    if arrived:
                        pe.wait_ge(s[arrived], 16)
                    transposes(n, lambda i: raw_w[:, (4 * n + i) * P:(4 * n + i + 1) * P], 4)

                def f_job(m, bank, src, n=4):
                    for i in range(n):
                        last = pe.transpose(bank[:, i * P:(i + 1) * P], src(i), ident[:])
                    last.then_inc(s["kvt_pe"], 1)

                pe.wait_ge(s["lat_ready"], 1)
                for m in range(2):
                    pe.wait_ge(s["tr_act"], NW - 3 + m)
                    f_job(m, psS[:, m, :], lambda i: lat1[:, 4 * m + i, :])

                def ctx_job(m, bank, par):
                    pe.wait_ge(s["norm_ready"], m - 1)
                    f_job(m, bank, lambda i: normed[:, par * 512 + i * D:par * 512 + (i + 1) * D])

                def q_job(bank, pair, head, half):
                    w = (pair * 2 + head) * P
                    xs = LAT0 + half * 512
                    return three(bank, Wq[:, 0, ds(w, P)], Wq[:, 1, ds(w, P)], kv_hi[:, xs:xs + 512], kv_lo[:, xs:xs + 512])

                def k_job(bank, pair, c):
                    c0, n = kcols(c)
                    return three(bank[:, 0:n], Wk[:, 0, ds(pair * P, P)], Wk[:, 1, ds(pair * P, P)],
                                 kv_hi[:, ds(c0, n)], kv_lo[:, ds(c0, n)])

                def v_tile(bank, pair, c, i):
                    c0, _ = kcols(c)
                    return three(bank[:, i * P:(i + 1) * P], kv_hi[:, ds(c0 + i * P, P)], kv_lo[:, ds(c0 + i * P, P)],
                                 Wv[:, 0, ds(pair * P, P)], Wv[:, 1, ds(pair * P, P)])

                def v_job(bank, pair, c):
                    for i in range(kcols(c)[1] // P):
                        last = v_tile(bank, pair, c, i)
                    return last

                pe.wait_ge(s["tr_low"], NW)
                pe.wait_ge(s["kvt_low"], 2)
                for i in range(4):
                    if i < 2:
                        pe.wait_ge(s["kvt_act"], i + 1)
                    q_job(psS[:, i, :], 0, i // 2, i % 2).then_inc(s["job_pe"], 1)
                pe.wait_ge(s["norm_ready"], 1)
                pe.wait_ge(s["job_dve"], 3)
                f_job(2, psS[:, 2, :], lambda i: normed[:, i * D:(i + 1) * D], 3)
                pe.wait_ge(s["kvt_low"], 3)
                for i, (fn, c) in enumerate(((k_job, 0), (v_job, 0), (k_job, 1), (v_job, 1))):
                    pe.wait_ge(s["job_dve"], i + 1)
                    fn(psS[:, i, :], 0, c).then_inc(s["job_pe"], 1)
                if exact:
                    pe.wait_ge(s["job_dve"], 8)
                    with pe.Fori(0, (LOOPS - 2) // 2) as i:
                        for u in range(2):
                            g = i * 2 + u
                            pe.wait_ge(s["kvt_act"], g + 3)
                            ctx_job(g + 3, psS[:, u, :], (3 + u) % 2)
                            pe.wait_ge(s["kvt_low"], g + 3)
                            pe.wait_ge(s["job_dve"], g * 2 + 8)
                            k_job(psJ, 0, g + 2).then_inc(s["job_pe"], 1)
                            pe.wait_ge(s["job_dve"], g * 2 + 9)
                            v_job(psJ, 0, g + 2).then_inc(s["job_pe"], 1)
                    pe.wait_ge(s["kvt_low"], FSTEPS)
                    pe.wait_ge(s["job_dve"], PRE - 2)
                    k_job(psJ, 0, LOOPS).then_inc(s["job_pe"], 1)
                    pe.wait_ge(s["job_dve"], PRE - 1)
                    v_job(psJ, 0, LOOPS).then_inc(s["job_pe"], 1)

                def row_max(pair, head, jobs):
                    h = pair * 2 + head
                    slot = slot_of(head, pair) * NKC
                    qo = (pair % 2) * 2 * NQ + head * NQ
                    with pe.Fori(0, QB) as b:
                        pe.wait_ge(s["job_dve"], jobs)
                        def part(n, c0, width):
                            pe.wait_ge(s["max_dve"], n + 1)
                            pe.matmul(psJ[:, 0:width], Q[:, 0, ds(qo + b * P, P)], K[:, ds(c0 + slot, width)],
                                      start=True, stop=True).then_inc(s["max_pe"], 1)
                        n0 = h * MAXS + b * (LOOPS + 1)
                        part(n0, 0, 3 * P)
                        with pe.Fori(0, LOOPS) as g:
                            part(n0 + g + 1, g * 512 + 3 * P, 512)
                    n1 = h * MAXS + QB * (LOOPS + 1)
                    for half in range(2):
                        pe.wait_ge(s["max_dve"], n1 + 2 + half)
                        for i in range(4):
                            b = 4 * half + i
                            last = pe.matmul(psJ[0:1, i * P:(i + 1) * P], mq[:, b:b + 1], ident[:], start=True, stop=True)
                        last.then_inc(s["max_pe"], 1)
                    pe.wait_ge(s["max_dve"], n1 + 4)

                def scores(pair, head, t, par, v_step=None):
                    def v_tiles(which):
                        if v_step:
                            for i in which:
                                last = v_tile(psJ, *v_step[1:], i)
                            if 3 in which:
                                last.then_inc(s["job_pe"], 1)
                    n = pair * 2 * NT + head * NT + t
                    slot = slot_of(head, pair) * NKC
                    if v_step:
                        pe.wait_ge(s["job_dve"], v_step[0])
                    if not isinstance(n, int) or n >= 2:
                        pe.wait_ge(s["exp_done"], n - 1)
                    qo = (pair % 2) * 2 * NQ + head * NQ
                    k = K[:, ds(slot + t * P, P)]
                    for half in range(2):
                        bank = psS[:, 2 * par + half, :]
                        pe.matmul(bank, k, Q[:, 0, ds(qo + half * 512, 512)], start=True, stop=False)
                        v_tiles([0] if half == 0 else [2, 3])
                        last = pe.matmul(bank, k, Q[:, 1, ds(qo + half * 512, 512)], start=False, stop=not exact)
                        if exact:
                            last = pe.matmul(bank, kconst[:], mrow[:, half * 512:half * 512 + 512], start=False, stop=True)
                        if half == 0:
                            v_tiles([1])
                    last.then_inc(s["scores_done"], 1)

                def values(pair, head, t, buf, first=False, last_tile=False):
                    n = pair * 2 * NT + head * NT + t
                    pe.wait_ge(s["rest_done"], n + 1)
                    v0 = slot_of(head, pair) * NT * VS + t * VS
                    for b in range(QB):
                        if first and b % 3 == 0:
                            h = pair * 2 + head
                            pe.wait_ge(s["o_copied"], 1 if isinstance(h, int) and h == 0 else h * 3 + (b // 3 - 1))
                        hi = Pb[:, 2 * (buf * NQ + b * P) + 1:2 * (buf * NQ + (b + 1) * P):2]
                        lo = Pl[:, buf * NQ + b * P:buf * NQ + (b + 1) * P]
                        o = o_bank(b)
                        pe.matmul(o, hi, V[:, ds(v0, VW)], start=first and b % 3 == 0, stop=False, skip_group_check=True)
                        last = pe.matmul(o[:, 0:DH + 1], lo, V[:, ds(v0, DH + 1)], start=False, stop=last_tile,
                                         skip_group_check=True)
                    if last_tile:
                        last.then_inc(s["pv_done"], 1)

                def job(n, fn, *args):
                    pe.wait_ge(s["job_dve"], n)
                    fn(psJ, *args).then_inc(s["job_pe"], 1)

                def t_job(bank, pair, half):
                    pe.wait_ge(s["on_ready"], pair * 2 + 1)
                    for i in range(4):
                        last = pe.transpose(bank[:, i * P:(i + 1) * P],
                                            On[:, :, :].rearrange("p b q -> p (b q)")[:, ds(half * 512 + i * P, P)], ident[:])
                    return last

                def y_job(bank, pair, half):
                    for i in range(4):
                        q = half * 512 + i * P
                        last = three(bank[:, i * P:(i + 1) * P], OT[:, 0, ds(q, P)], OT[:, 1, ds(q, P)],
                                     Wo[:, 0, ds((pair - 1) * P, P)], Wo[:, 1, ds((pair - 1) * P, P)])
                    return last

                def group(pair, head, g, jobs=(), v_step=None):
                    for j in range(4):
                        for at, n, fn, args in jobs:
                            if at == j:
                                job(n, fn, *args)
                        scores(pair, head, g * 4 + (3 + j), (head + 3 + j) % 2, v_step if j == 3 else None)
                        values(pair, head, g * 4 + (1 + j), (1 + j) % 4)

                def first_group(g, par, fill):
                    for j in range(4):
                        if j == 1:
                            if fill:
                                pe.wait_ge(s["exp_done"], g * 4 + 3)
                                ctx_job(g + 3, psS[:, 0, :], par)
                            pe.wait_ge(s["kvt_low"], g + 3)
                            job(g * 2 + 8, k_job, 0, g + 2)
                            values(0, 0, g * 4 + 2, 2)
                            if fill:
                                pe.wait_ge(s["kvt_act"], g + 4)
                        scores(0, 0, g * 4 + (3 + j), (3 + j) % 2, (g * 2 + 9, 0, g + 2) if j == 3 else None)
                        if j != 1:
                            values(0, 0, g * 4 + (1 + j), (1 + j) % 4)

                def body(pair, head, last_pair):
                    base = job0(pair)
                    scores(pair, head, 2, head)
                    if head == 1 and not last_pair:
                        job(base + JOBS_A + 1, v_job, pair + 1, 0)
                    values(pair, head, 0, 0, first=True)
                    if head == 0 and isinstance(pair, int) and pair == 0:
                        if exact:
                            with pe.Fori(0, LOOPS - 1) as g:
                                group(0, 0, g)
                        else:
                            with pe.Fori(0, (LOOPS - 2) // 2) as i:
                                for u in range(2):
                                    first_group(i * 2 + u, (3 + u) % 2, True)
                            first_group(LOOPS - 2, 0, False)
                        group(0, 0, LOOPS - 1, [(i, PRE + i, q_job, (1, i // 2, i % 2)) for i in range(4)])
                    elif head == 0:
                        for u in range(2):
                            group(pair, 0, u * 2, [(1, base + u * 2, t_job, (pair, u))])
                            group(pair, 0, u * 2 + 1, [(1, base + u * 2 + 1, y_job, (pair, u))])
                        if not last_pair:
                            with pe.Fori(0, 2) as u:
                                for half in range(2):
                                    group(pair, 0, u * 2 + (4 + half), [(1, base + u * 2 + (4 + half), q_job, (pair + 1, u, half))])
                        with pe.Fori(4 if last_pair else 8, LOOPS) as g:
                            group(pair, 0, g)
                    else:
                        with pe.Fori(0, LOOPS) as g:
                            n = base + JOBS_A + 2 + g * 2
                            if last_pair:
                                group(pair, 1, g)
                            else:
                                group(pair, 1, g, [(1, n, k_job, (pair + 1, g + 1))], (n + 1, pair + 1, g + 1))
                    nxt = (pair, 1) if head == 0 else (pair + 1, 0)
                    more = not (last_pair and head == 1)
                    for t in range(2):
                        if more:
                            if t == 0:
                                if exact:
                                    row_max(*nxt, base + 4 if last_pair else base + (JOBS_A if head == 0 else JOBS))
                            if t == 0 and head == 0 and not last_pair:
                                job(base + JOBS_A, k_job, pair + 1, 0)
                            scores(*nxt, t, (nxt[1] + t) % 2)
                        values(pair, head, NT - 2 + t, (NT - 2 + t) % 4, last_tile=t == 1)

                if exact:
                    row_max(0, 0, PRE)
                pe.wait_ge(s["job_dve"], 6)
                scores(0, 0, 0, 0)
                pe.wait_ge(s["job_dve"], 8)
                scores(0, 0, 1, 1)
                body(0, 0, False)
                body(0, 1, False)
                with pe.Fori(1, PAIRS - 1) as p:
                    body(p, 0, False)
                    body(p, 1, False)
                body(PAIRS - 1, 0, True)
                body(PAIRS - 1, 1, True)
                base = job0(PAIRS - 1) + 4
                pe.wait_ge(s["exp_done"], HEADS * NT)
                for u in range(2):
                    t_job(psS[:, u, :], PAIRS, u).then_inc(s["job_pe"], 1)
                pe.wait_ge(s["job_dve"], base)
                pe.matmul(psJ[0:1, 0:QB], ones[:, 0:1], good[:, 0, :], start=True, stop=True).then_inc(s["good_sum"], 1)
                for u in range(2):
                    pe.wait_ge(s["job_dve"], base + 1 + u)
                    y_job(psS[:, 2 + u, :], PAIRS, u).then_inc(s["job_pe"], 1)

            attention(runs[0], False)
            pe.wait_ge(runs[0]["flag_ready"], 1)
            again = pe.value_load(flag[0:1, 0:1], min_val=0, max_val=1)
            with pe.If(again > 0):
                attention(runs[1], True)
                pe.nop()

            for half in range(2):
                pe.wait_ge(f["xt"], half + 1)
                for i in range(4):
                    last = pe.transpose(psS[:, half, i * P:(i + 1) * P], lat1[:, 4 * half + i, :], ident[:])
                last.then_inc(f["xt_t"], 1)
            pe.wait_ge(f["xt_split"], 2)
            for b in range(QB):
                t = [xt16[i][:, b * P:(b + 1) * P] for i in range(2)]
                last = three(psX[:, 3, b * E:(b + 1) * E], t[0], t[1], gate_hl[:, 0, :], gate_hl[:, 1, :])
            last.then_inc(f["gate_pe"], 1)

            def hidden(n, e, j):
                if not isinstance(n, int) or n >= 2:
                    pe.wait_ge(f["gelu"], n - 1)
                c = e * HID + j * P
                for half in range(2):
                    xs = half * 512
                    last = three(psS[:, 2 * (j % 2) + half, :], W1[0][:, ds(c, P)], W1[1][:, ds(c, P)],
                                 xt16[0][:, xs:xs + 512], xt16[1][:, xs:xs + 512])
                last.then_inc(f["h_pe"], 1)

            def mix(n, e, j, par):
                pe.wait_ge(f["rest"], n + 1)
                c = e * HID + j * P
                for b in range(QB):
                    hi = Pb[:, 2 * (j * NQ + b * P) + 1:2 * (j * NQ + (b + 1) * P):2]
                    lo = Pl[:, j * NQ + b * P:j * NQ + (b + 1) * P]
                    o = psX[:, 2 * par + b // 4, (b % 4) * P:(b % 4 + 1) * P]
                    pe.matmul(o, hi, W2[0][:, ds(c, P)], start=j == 0 and b % 4 == 0, stop=False, skip_group_check=True)
                    pe.matmul(o, hi, W2[1][:, ds(c, P)], start=False, stop=False, skip_group_check=True)
                    last = pe.matmul(o, lo, W2[0][:, ds(c, P)], start=False, stop=j == HT - 1, skip_group_check=True)
                last.then_inc(f["mix"], 1)

            hidden(0, 0, 0)
            hidden(1, 0, 1)

            def gate_rows():
                pe.wait_ge(f["gates"], 1)
                for half in range(2):
                    for i in range(4):
                        last = pe.transpose(psX[0:E, 2 + half, i * P:(i + 1) * P], gates[:, 0, 4 * half + i, :], ident[:])
                last.then_inc(f["wt_pe"], 1)

            def offsets():
                pe.wait_ge(f["wt_c"], 2)
                pe.wait_ge(f["b2_in"], 16)
                for b in range(QB):
                    last = pe.matmul(psX[:, 2 + b // 4, (b % 4) * P:(b % 4 + 1) * P], wT[:, b * P:(b + 1) * P], b2s[:],
                                     start=True, stop=True)
                last.then_inc(f["b2_pe"], 1)

            def two_experts(e, last):
                for par in range(2):
                    for j in range(HT):
                        n = (e + par) * HT + j
                        if j == 0 and not (isinstance(e, int) and e + par == 0):
                            pe.wait_ge(f["y_dve"], e + par)
                        if not (last and par == 1 and j >= 2):
                            hidden(n + 2, e + par + (j >= 2), (j + 2) % HT)
                        mix(n, e + par, j, par)
                        if isinstance(e, int) and n == 1:
                            gate_rows()
                        if isinstance(e, int) and n == 2:
                            offsets()

            two_experts(0, False)
            with pe.Fori(1, E // 2 - 1) as i:
                two_experts(i * 2, False)
            two_experts(E - 2, True)

        @block.scalar
        def _(act):
            def attention(s, exact):
                act.wait_ge(cst, N_CST)
                act.wait_ge(s["par_t"], 1)
                act.activation(parT[:, 0:ROWS], psJ[:, 0:ROWS], ACT.Copy).then_inc(s["par_c"], 1)

                roots = [0]

                def root(i, n):
                    roots[0] += 1
                    act.wait_ge(s["var_ready"], roots[0])
                    act.activation(rs[:, i:i + n], mv[:, i:i + n, 1], ACT.Sqrt, bias=consts[:, 0:1]).then_inc(s["sqrt_ready"], 1)

                def weights(n):
                    act.wait_ge(s["tr_pe"], n + 1)
                    src = psS[:, n % 4, :]
                    if n < 2:
                        for twin in range(2):
                            dst = Wq[:, 0, n * 1024:(n + 1) * 1024].rearrange("p (h t d) -> p h t d", t=2, d=DH)[:, :, twin, :]
                            act.activation(dst, src.rearrange("p (h d) -> p h d", d=DH), ACT.Copy, scale=WS)
                    else:
                        w, o = (Wk, Wv, Wo)[n // 2 - 1], (n % 2) * 512
                        act.activation(w[:, 0, o:o + 512], src, ACT.Copy, scale=WS)
                    act.activation(evac_w[:, n * 512:(n + 1) * 512], src, ACT.Copy, scale=WS).then_inc(s["tr_act"], 1)

                weights(0)
                root(ST_X, QB)
                weights(1)
                weights(2)
                root(ST_LAT, QB)
                for n in range(3, NW):
                    weights(n)

                def split_kv(m, bank, par, scale, offset):
                    act.wait_ge(s["kvt_pe"], m + 1)
                    if not (isinstance(m, int) and m < 2):
                        act.wait_ge(s["kvt_low"], m - 1)
                    cols = fcols(m)
                    for c0, o, n in cols if isinstance(m, int) and m <= 2 else ():
                        act.activation(kv_hi[:, ds(c0, n)], bank[:, o:o + n], ACT.Identity, bias=offset, scale=scale)
                    n = sum(n for _, _, n in cols)
                    act.activation(evac[:, par * 512:par * 512 + n], bank[:, 0:n], ACT.Identity, bias=offset,
                                   scale=scale).then_inc(s["kvt_act"], 1)

                def split_ctx(m, bank, par):
                    split_kv(m, bank, par, parT[:, R_LN1W:R_LN1W + 1], parT[:, R_LN1B:R_LN1B + 1])

                act.wait_ge(s["par_c"], 3)
                for m in range(2):
                    split_kv(m, psS[:, m, :], m, aff[:, 0:1], aff[:, 1:2])
                root(ST_CTX, CHUNKS[0][1])

                def q_part(bank, pair, head, half):
                    act.activation(Q[:, 0, ds((pair % 2) * 2 * NQ + head * NQ + half * 512, 512)], bank, ACT.Copy)\
                       .then_inc(s["job_act"], 1)

                def k_part(bank, pair, c):
                    c0, n = kcols(c)
                    act.activation(K[0:DH, ds(A_SLOT * NKC + c0, n)], bank[0:DH, 0:n], ACT.Copy)
                    act.activation(K[DH:P, ds(slot_of(1, pair) * NKC + c0, n)], bank[DH:P, 0:n], ACT.Copy)\
                       .then_inc(s["job_act"], 1)

                def v_part(bank, pair, c):
                    first = isinstance(c, int) and c == 0
                    t0, n = (0, 3) if first else (c * 4 - 1, 4)
                    src = bank.rearrange("p (t d) -> p t d", d=P)
                    for head in range(2):
                        v0 = slot_of(head, pair) * NT * VS
                        if first:
                            act.activation(V[:, ds(v0, DH)], src[:, 0, head * DH:head * DH + DH], ACT.Copy, scale=mask[:, 0:1])
                        a = 1 if first else 0
                        dst = V[:, ds(v0 + (t0 + a) * VS, (n - a) * VS)].rearrange("p (t w) -> p t w", w=VS)[:, :, 0:DH]
                        last = act.activation(dst, src[:, a:n, head * DH:head * DH + DH], ACT.Copy)
                    last.then_inc(s["job_act"], 1)

                def pre(n, fn, *args):
                    act.wait_ge(s["job_pe"], n + 1)
                    fn(*args)

                for i in range(4):
                    pre(i, q_part, psS[:, i, :], 0, i // 2, i % 2)
                split_ctx(2, psS[:, 2, :], 0)
                pre(4, k_part, psS[:, 0, :], 0, 0)
                pre(5, v_part, psS[:, 1, :], 0, 0)
                pre(6, k_part, psS[:, 2, :], 0, 1)
                pre(7, v_part, psS[:, 3, :], 0, 1)
                root(ST_CTX + CHUNKS[1][0], CHUNKS[1][1])
                if exact:
                    with act.Fori(0, (LOOPS - 2) // 2) as i:
                        for u in range(2):
                            g = i * 2 + u
                            split_ctx(g + 3, psS[:, u, :], (3 + u) % 2)
                            pre(g * 2 + 8, k_part, psJ, 0, g + 2)
                            pre(g * 2 + 9, v_part, psJ, 0, g + 2)
                    pre(PRE - 2, k_part, psJ, 0, LOOPS)
                    pre(PRE - 1, v_part, psJ, 0, LOOPS)

                def exp(pair, head, t, par, buf):
                    act.wait_ge(s["scores_done"], pair * 2 * NT + head * NT + t + 1)
                    act.activation(Pf[:, buf * NQ:(buf + 1) * NQ], psS[:, 2 * par:2 * par + 2, :].rearrange("p a n -> p (a n)"),
                                   ACT.Exp, bias=consts[:, 1:2], scale=EXP_SCALE).then_inc(s["exp_done"], 1)

                def job(n, fn, *args):
                    act.wait_ge(s["job_pe"], n + 1)
                    fn(psJ, *args)

                def t_part(bank, half):
                    act.activation(OT[:, 0, ds(half * 512, 512)], bank, ACT.Copy).then_inc(s["job_act"], 1)

                def group(pair, head, g, jobs=()):
                    for j in range(4):
                        for at, n, fn, args in jobs:
                            if at == j:
                                job(n, fn, *args)
                        exp(pair, head, g * 4 + (3 + j), (head + 3 + j) % 2, (3 + j) % 4)

                def first_group(g, par, fill):
                    if fill:
                        split_ctx(g + 3, psS[:, 0, :], par)
                    group(0, 0, g, [(1, g * 2 + 8, k_part, (0, g + 2)), (3, g * 2 + 9, v_part, (0, g + 2))])

                def copy_out(pair, head):
                    act.wait_ge(s["pv_done"], pair * 2 + head + 1)
                    act.wait_ge(s["on_ready"], pair * 2 + head + 1)
                    for b in range(3):
                        n = min(3, QB - 3 * b)
                        act.activation(Oraw[:, 3 * b:3 * b + n, :].rearrange("p b w -> p (b w)"), psX[:, b, 0:n * VW], ACT.Copy)\
                            .then_inc(s["o_copied"], 1)

                def body(pair, head, last_pair):
                    base = job0(pair)
                    if head == 1 and not last_pair:
                        job(base + JOBS_A + 1, v_part, pair + 1, 0)
                    exp(pair, head, 2, (head + 2) % 2, 2)
                    if head == 0 and isinstance(pair, int) and pair == 0:
                        if exact:
                            with act.Fori(0, LOOPS - 1) as g:
                                group(0, 0, g)
                        else:
                            with act.Fori(0, (LOOPS - 2) // 2) as i:
                                for u in range(2):
                                    first_group(i * 2 + u, (3 + u) % 2, True)
                            first_group(LOOPS - 2, 0, False)
                        group(0, 0, LOOPS - 1, [(i, PRE + i, q_part, (1, i // 2, i % 2)) for i in range(4)])
                    elif head == 0:
                        for u in range(2):
                            group(pair, 0, u * 2, [(1, base + u * 2, t_part, (u,))])
                            group(pair, 0, u * 2 + 1)
                        if not last_pair:
                            with act.Fori(0, 2) as u:
                                for half in range(2):
                                    group(pair, 0, u * 2 + (4 + half), [(1, base + u * 2 + (4 + half), q_part, (pair + 1, u, half))])
                        with act.Fori(4 if last_pair else 8, LOOPS) as g:
                            group(pair, 0, g)
                    elif not last_pair:
                        with act.Fori(0, LOOPS) as g:
                            n = base + JOBS_A + 2 + g * 2
                            group(pair, 1, g, [(1, n, k_part, (pair + 1, g + 1)), (3, n + 1, v_part, (pair + 1, g + 1))])
                    else:
                        with act.Fori(0, 6) as g:
                            group(pair, 1, g)
                        act.wait_ge(s["ffnw_in"], 32)
                        for raw, w in ((raw_w1, W1), (raw_w2, W2)):
                            g0 = 6 if raw is raw_w1 else 10
                            with act.Fori(0, 4) as g:
                                group(pair, 1, g + g0)
                                act.activation(w[0][:, ds(g * NQ, NQ)], raw[:, ds(g * NQ, NQ)], ACT.Copy, scale=WS)\
                                   .then_inc(s["wh_done"], 1)
                    if not (last_pair and head == 1):
                        nxt = (pair, 1) if head == 0 else (pair + 1, 0)
                        if head == 0 and not last_pair:
                            job(base + JOBS_A, k_part, pair + 1, 0)
                        for t in range(2):
                            exp(*nxt, t, (nxt[1] + t) % 2, t)
                    copy_out(pair, head)

                exp(0, 0, 0, 0, 0)
                exp(0, 0, 1, 1, 1)
                body(0, 0, False)
                body(0, 1, False)
                with act.Fori(1, PAIRS - 1) as p:
                    body(p, 0, False)
                    body(p, 1, False)
                body(PAIRS - 1, 0, True)
                body(PAIRS - 1, 1, True)
                base = job0(PAIRS - 1) + 4
                for u in range(2):
                    act.wait_ge(s["job_pe"], base + u + 1)
                    t_part(psS[:, u, :], u)

            attention(runs[0], False)
            act.wait_ge(runs[0]["flag_ready"], 1)
            again = act.value_load(flag[0:1, 0:1], min_val=0, max_val=1)
            with act.If(again > 0):
                attention(runs[1], True)
                act.nop()

            act.activation(gate_hl[:, 0, :], parT[:, R_GATE:R_GATE + E], ACT.Copy, scale=WS).then_inc(f["gw_high"], 1)
            act.wait_ge(f["var"], 1)
            act.activation(rs[:, 0:QB], mv[:, 0:QB, 1], ACT.Sqrt, bias=consts[:, 0:1]).then_inc(f["sqrt"], 1)
            for half in range(2):
                act.wait_ge(f["xt_t"], half + 1)
                act.activation(xt16[0][:, half * 512:half * 512 + 512], psS[:, half, :], ACT.Copy).then_inc(f["xt_c"], 1)
            act.wait_ge(f["shifted"], 1)
            act.activation(gates[:, 1, :, :], gates[:, 1, :, :], ACT.Exp, scale=1.0 / WS).then_inc(f["gexp"], 1)

            def gelu(n, e, j):
                act.wait_ge(f["h_pe"], n + 1)
                if not isinstance(n, int) or n >= 4:
                    act.wait_ge(f["mix"], n - 3)
                act.activation(Pf[:, j * NQ:(j + 1) * NQ],
                               psS[:, 2 * (j % 2):2 * (j % 2) + 2, :].rearrange("p a n -> p (a n)"), ACT.Gelu,
                               bias=parT[:, ds(R_B1 + e * HT + j, 1)], scale=1.0 / WS).then_inc(f["gelu"], 1)

            for j in range(HT):
                gelu(j, 0, j)
            with act.Fori(1, E) as e:
                for j in range(HT):
                    gelu(e * HT + j, e, j)

        @block.vector
        def _(dve):
            def attention(s, exact):
                count = [0]

                def link(ins):
                    ins.then_inc(s["dve_chain"], 1)
                    count[0] += 1
                    dve.wait_ge(s["dve_chain"], count[0])

                roots = [0]

                def variances(i, src, n, done=0):
                    for k in range(done, n):
                        last = dve.bn_stats(stats[:, i + k, :], src(k))
                    link(last)
                    for k in range(n):
                        last = dve.bn_aggr(mv[:, i + k, :], stats[:, i + k, :])
                    last.then_inc(s["var_ready"], 1)

                def inv_std(i, n):
                    roots[0] += 1
                    dve.wait_ge(s["sqrt_ready"], roots[0])
                    newton(dve, link, rs[:, i:i + n], rt[:, i:i + n], mv[:, i:i + n, 1])

                def normalise(i, n, src, dst):
                    for k in range(n):
                        last = dve.tensor_scalar(dst(k), src(k), mv[:, i + k, 0:1], rs[:, i + k:i + k + 1], ALU.subtract, ALU.mult)
                    return last

                def ones_of(slot):
                    ones_col = V[:, slot * NT * VS:(slot + 1) * NT * VS].rearrange("p (t w) -> p t w", w=VS)[:, :, DH:DH + 1]
                    link(dve.memset(ones_col, 1.0))
                    return dve.tensor_copy(ones_col[:, 0, :], mask[:])

                dve.wait_ge(cst, N_CST)
                ones_of(0)
                ones_of(1)
                dve.wait_ge(s["x_in"], 16)
                variances(ST_X, lambda k: y[:, k, :], QB)
                inv_std(ST_X, QB)
                link(normalise(ST_X, QB, lambda k: y[:, k, :], lambda k: lat0[:, k, :]))
                variances(ST_LAT, lambda k: lat0[:, k, :], QB)
                inv_std(ST_LAT, QB)
                normalise(ST_LAT, QB, lambda k: lat0[:, k, :], lambda k: lat1[:, k, :]).then_inc(s["lat_ready"], 1)
                dve.wait_ge(s["par_c"], 1)
                link(dve.tensor_scalar(rden[:, 0:1], parT[:, R_COND:R_COND + 1], 1.0, None, ALU.add))
                dve.tensor_tensor(aff[:, 0:1], parT[:, R_LN2W:R_LN2W + 1], rden[:, 0:1], ALU.mult).then_inc(s["par_c"], 1)
                dve.scalar_tensor_tensor(aff[:, 1:2], parT[:, R_LN2B:R_LN2B + 1], rden[:, 0:1], parT[:, R_COND:R_COND + 1],
                                         ALU.mult, ALU.add).then_inc(s["par_c"], 1)

                def ctx_var(c, done):
                    t0, n = CHUNKS[c]
                    variances(ST_CTX + t0, lambda k: raw_tile(t0 + k), n, done)

                def ctx_rs(c):
                    inv_std(ST_CTX + CHUNKS[c][0], CHUNKS[c][1])
                    dve.memset(mq[:, c:c + 1], 0.0).then_inc(s["rs_ready"], 1)

                def ctx_stats(c, a, b):
                    for k in range(CHUNKS[c][0] + a, CHUNKS[c][0] + b):
                        dve.bn_stats(stats[:, ST_CTX + k, :], raw_tile(k))

                dve.wait_ge(s["ctx_in0"], 32)
                ctx_stats(0, 0, CHUNKS[0][1] - 1)
                for m in range(2):
                    dve.wait_ge(s["kvt_act"], m + 1)
                    c = LAT0 + m * 512
                    dve.tensor_tensor(kv_lo[:, c:c + 512], evac[:, m * 512:m * 512 + 512], kv_hi[:, c:c + 512], ALU.subtract)\
                        .then_inc(s["kvt_low"], 1)
                ctx_var(0, CHUNKS[0][1] - 1)
                dve.wait_ge(s["kvt_pe"], 2)
                dve.memset(rden[:, :], 0.0).then_inc(s["on_ready"], 1)
                dve.memset(good[:, 0, :], 0.0).then_inc(s["o_copied"], 1)
                ctx_rs(0)

                def q_part(bank, pair, head, half):
                    o = (pair % 2) * 2 * NQ + head * NQ + half * 512
                    dve.tensor_tensor(Q[:, 1, ds(o, 512)], bank, Q[:, 0, ds(o, 512)], ALU.subtract).then_inc(s["job_dve"], 1)

                def k_part(bank, pair, c):
                    c0, n = kcols(c)
                    a, b = ds(A_SLOT * NKC + c0, n), ds(slot_of(1, pair) * NKC + c0, n)
                    dve.tensor_tensor(K[DH:P, a], bank[0:DH, 0:n], K[0:DH, a], ALU.subtract)
                    dve.tensor_tensor(K[0:DH, b], bank[DH:P, 0:n], K[DH:P, b], ALU.subtract).then_inc(s["job_dve"], 1)

                def v_part(bank, pair, c):
                    first = isinstance(c, int) and c == 0
                    t0, n = (0, 3) if first else (c * 4 - 1, 4)
                    src = bank.rearrange("p (t d) -> p t d", d=P)
                    for head in range(2):
                        v0 = slot_of(head, pair) * NT * VS
                        if first:
                            dve.scalar_tensor_tensor(V[:, ds(v0 + DH + 1, DH)], src[:, 0, head * DH:head * DH + DH], mask[:, 0:1],
                                                     V[:, ds(v0, DH)], ALU.mult, ALU.subtract)
                        a = 1 if first else 0
                        v = V[:, ds(v0 + (t0 + a) * VS, (n - a) * VS)].rearrange("p (t w) -> p t w", w=VS)
                        last = dve.tensor_tensor(v[:, :, DH + 1:VW], src[:, a:n, head * DH:head * DH + DH], v[:, :, 0:DH],
                                                 ALU.subtract)
                    last.then_inc(s["job_dve"], 1)

                def pre(n, fn, *args):
                    dve.wait_ge(s["job_act"], n + 1)
                    fn(*args)

                dve.wait_ge(s["ctx_in1"], 16)
                done = 0
                for i in range(4):
                    n = 3 if i < 3 else 8
                    pre(i, q_part, psS[:, i, :], 0, i // 2, i % 2)
                    ctx_stats(1, done, done + n)
                    done += n
                pre(4, k_part, psS[:, 0, :], 0, 0)
                pre(5, v_part, psS[:, 1, :], 0, 0)
                ctx_var(1, done)
                pre(6, k_part, psS[:, 2, :], 0, 1)
                pre(7, v_part, psS[:, 3, :], 0, 1)
                ctx_rs(1)
                if exact:
                    with dve.Fori(0, LOOPS - 1) as g:
                        pre(g * 2 + 8, k_part, psJ, 0, g + 2)
                        pre(g * 2 + 9, v_part, psJ, 0, g + 2)

                def rest(pair, head, t, buf):
                    dve.wait_ge(s["exp_done"], pair * 2 * NT + head * NT + t + 1)
                    dve.tensor_tensor(Pl[:, buf * NQ:(buf + 1) * NQ], Pf[:, buf * NQ:(buf + 1) * NQ],
                                      Pb[:, 2 * buf * NQ + 1:2 * (buf + 1) * NQ:2], ALU.subtract).then_inc(s["rest_done"], 1)

                def row_max(pair, head):
                    h = pair * 2 + head
                    with dve.Fori(0, QB) as b:
                        def part(n, i, width):
                            dve.wait_ge(s["max_pe"], n + 1)
                            dve.tensor_reduce(chunk_max[:, ds(b * (LOOPS + 1) + i, 1)], psJ[:, 0:width], AX_X, ALU.max)\
                               .then_inc(s["max_dve"], 1)
                        n0 = h * MAXP + b * (LOOPS + 1)
                        part(n0, 0, 3 * P)
                        with dve.Fori(0, LOOPS) as g:
                            part(n0 + g + 1, g + 1, 512)
                    done = h * MAXS + QB * (LOOPS + 1) + 1
                    dve.wait_ge(s["max_dve"], done)
                    dve.tensor_reduce(mq[:, :], chunk_max[:, :].rearrange("p (b c) -> p b c", b=QB), AX_X, ALU.max)\
                       .then_inc(s["max_dve"], 1)
                    for half in range(2):
                        dve.wait_ge(s["max_pe"], h * MAXP + QB * (LOOPS + 1) + 1 + half)
                        dve.tensor_scalar(mrow[:, half * 512:half * 512 + 512], psJ[0:1, :], -1.0 / MROW, None, ALU.mult)\
                           .then_inc(s["max_dve"], 1)

                def job(n, needs_act, fn, *args):
                    if needs_act is None:
                        dve.wait_ge(s["job_pe"], n + 1)
                    else:
                        dve.wait_ge(s["job_act"], needs_act + 1)
                    fn(psJ, *args)

                def t_part(bank, half):
                    dve.tensor_tensor(OT[:, 1, ds(half * 512, 512)], bank, OT[:, 0, ds(half * 512, 512)], ALU.subtract)\
                       .then_inc(s["job_dve"], 1)

                def y_part(bank, half, n):
                    o = y[:, :, :].rearrange("p b d -> p (b d)")[:, ds(half * 512, 512)]
                    dve.wait_ge(s["job_dve"], n)
                    dve.scalar_tensor_tensor(o, bank, 1.0 / (WS * WS), o, ALU.mult, ALU.add).then_inc(s["job_dve"], 1)

                def group(pair, head, g, jobs=()):
                    for j in range(4):
                        for at, n, na, fn, args in jobs:
                            if at == j:
                                job(n, na, fn, *args)
                        rest(pair, head, g * 4 + (3 + j), (3 + j) % 4)

                LINKS = 5

                def combine(pair, head):
                    h = pair * 2 + head
                    n0 = h * LINKS + links0
                    dve.wait_ge(s["o_copied"], h * 3 + 4)
                    dve.wait_ge(s["dve_chain"], n0)
                    den = Oraw[:, :, DH]
                    dve.tensor_scalar(good[:, 1, :], den, SUM_MIN, None, ALU.is_ge).then_inc(s["dve_chain"], 1)
                    dve.reciprocal(rden[:, :], den).then_inc(s["dve_chain"], 1)
                    dve.tensor_tensor(Oraw[:, :, 0:DH], Oraw[:, :, 0:DH], Oraw[:, :, DH + 1:VW], ALU.add)\
                       .then_inc(s["dve_chain"], 1)
                    dve.wait_ge(s["dve_chain"], n0 + 1)
                    dve.scalar_tensor_tensor(good[:, 2, :], den, SUM_MAX, good[:, 1, :], ALU.is_le, ALU.mult)\
                       .then_inc(s["dve_chain"], 1)
                    dve.wait_ge(s["dve_chain"], n0 + 4)
                    dve.tensor_tensor(good[:, 0, :], good[:, 0, :], good[:, 2, :], ALU.add).then_inc(s["dve_chain"], 1)
                    dve.tensor_tensor(On[:, :, head * DH:head * DH + DH], Oraw[:, :, 0:DH],
                                      rden[:, :].unsqueeze(2).to_broadcast([P, QB, DH]), ALU.mult)\
                       .then_inc(s["on_ready"], 1)

                def body(pair, head, last_pair):
                    base, ab = job0(pair), act0(pair)
                    if head == 1 and not last_pair:
                        job(None, ab + ACT_A + 1, v_part, pair + 1, 0)
                    rest(pair, head, 2, 2)
                    if head == 1 and not last_pair:
                        combine(pair, 0)
                    if head == 0 and isinstance(pair, int) and pair == 0:
                        with dve.Fori(0, LOOPS - 1) as g:
                            group(0, 0, g, () if exact else [(1, None, g * 2 + 8, k_part, (0, g + 2)),
                                                             (3, None, g * 2 + 9, v_part, (0, g + 2))])
                        group(0, 0, LOOPS - 1, [(i, None, PRE + i, q_part, (1, i // 2, i % 2)) for i in range(4)])
                        ones_of(2)
                    elif head == 0:
                        for u in range(2):
                            group(pair, 0, u * 2, [(1, None, ab + u, t_part, (u,))])
                            group(pair, 0, u * 2 + 1, [(1, base + u * 2 + 1, None, y_part, (u, base + u * 2 + 1))])
                        if not last_pair:
                            with dve.Fori(0, 2) as u:
                                for half in range(2):
                                    group(pair, 0, u * 2 + (4 + half), [(1, None, ab + u * 2 + (2 + half), q_part, (pair + 1, u, half))])
                        with dve.Fori(4 if last_pair else 8, LOOPS) as g:
                            group(pair, 0, g)
                    elif not last_pair:
                        with dve.Fori(0, LOOPS) as g:
                            n = ab + ACT_A + 2 + g * 2
                            group(pair, 1, g, [(1, None, n, k_part, (pair + 1, g + 1)), (3, None, n + 1, v_part, (pair + 1, g + 1))])
                    else:
                        with dve.Fori(0, 6) as g:
                            group(pair, 1, g)
                        for k, (raw, w) in enumerate(((raw_w1, W1), (raw_w2, W2))):
                            with dve.Fori(0, 4) as g:
                                group(pair, 1, g + (6 + 4 * k))
                                dve.wait_ge(s["wh_done"], g + (4 * k + 1))
                                dve.scalar_tensor_tensor(w[1][:, ds(g * NQ, NQ)], raw[:, ds(g * NQ, NQ)], WS,
                                                         w[0][:, ds(g * NQ, NQ)], ALU.mult, ALU.subtract).then_inc(s["wl_done"], 1)
                    if not (last_pair and head == 1):
                        nxt = (pair, 1) if head == 0 else (pair + 1, 0)
                        if exact:
                            row_max(*nxt)
                        if head == 0 and not last_pair:
                            job(None, ab + ACT_A, k_part, pair + 1, 0)
                        for t in range(2):
                            rest(*nxt, t, t)
                    if head == 1 or last_pair:
                        combine(pair, head)

                links0 = count[0] + 1
                if exact:
                    dve.memset(mq[:, :], 0.0).then_inc(s["max_dve"], 1)
                    row_max(0, 0)
                rest(0, 0, 0, 0)
                rest(0, 0, 1, 1)
                body(0, 0, False)
                body(0, 1, False)
                with dve.Fori(1, PAIRS - 1) as p:
                    body(p, 0, False)
                    body(p, 1, False)
                body(PAIRS - 1, 0, True)
                body(PAIRS - 1, 1, True)
                base, ab = job0(PAIRS - 1) + 4, act0(PAIRS - 1) + 2
                for u in range(2):
                    dve.wait_ge(s["job_act"], ab + u + 1)
                    t_part(psS[:, u, :], u)
                dve.wait_ge(s["good_sum"], 1)
                dve.tensor_reduce(total[:], psJ[0:1, 0:QB], AX_X, ALU.add).then_inc(s["total_ready"], 1)
                dve.wait_ge(s["total_ready"], 1)
                dve.tensor_scalar(flag[:], total[:], float(HEADS * NQ), None, ALU.is_lt).then_inc(s["flag_ready"], 1)
                for u in range(2):
                    dve.wait_ge(s["job_pe"], base + 3 + u)
                    y_part(psS[:, 2 + u, :], u, base + 2 + u)
                dve.wait_ge(s["job_dve"], base + 4)

            attention(runs[0], False)
            dve.wait_ge(runs[0]["flag_ready"], 1)
            again = dve.value_load(flag[0:1, 0:1], min_val=0, max_val=1)
            with dve.If(again > 0):
                attention(runs[1], True)
                dve.nop()

            count = [0]

            def link(ins):
                ins.then_inc(f["chain"], 1)
                count[0] += 1
                dve.wait_ge(f["chain"], count[0])

            for k in range(QB):
                last = dve.bn_stats(stats[:, k, :], y[:, k, :])
            link(last)
            for k in range(QB):
                last = dve.bn_aggr(mv[:, k, :], stats[:, k, :])
            last.then_inc(f["var"], 1)
            dve.wait_ge(f["gw_high"], 1)
            dve.scalar_tensor_tensor(gate_hl[:, 1, :], parT[:, R_GATE:R_GATE + E], WS, gate_hl[:, 0, :], ALU.mult, ALU.subtract)
            dve.wait_ge(f["sqrt"], 1)
            newton(dve, link, rs[:, 0:QB], rt[:, 0:QB], mv[:, 0:QB, 1])
            for half in range(2):
                for k in range(4 * half, 4 * half + 4):
                    last = dve.tensor_scalar(lat1[:, k, :], y[:, k, :], mv[:, k, 0:1], rs[:, k:k + 1], ALU.subtract, ALU.mult)
                last.then_inc(f["xt"], 1)
            for half in range(2):
                dve.wait_ge(f["xt_c"], half + 1)
                h = slice(half * 512, half * 512 + 512)
                dve.tensor_tensor(xt16[1][:, h], psS[:, half, :], xt16[0][:, h], ALU.subtract).then_inc(f["xt_split"], 1)

            def g(i):
                return gates[:, i, :, :]

            def wide(a):
                return a.unsqueeze(2).to_broadcast([P, QB, E])

            def sm(i):
                return small[:, i, :]

            dve.wait_ge(f["gate_pe"], 1)
            logits = psX[:, 3, 0:QB * E].rearrange("p (b e) -> p b e", e=E)
            link(dve.tensor_reduce(sm(0), logits, AX_X, ALU.max))
            dve.tensor_tensor(g(1), logits, wide(sm(0)), ALU.subtract).then_inc(f["shifted"], 1)

            def rest(n, j):
                dve.wait_ge(f["gelu"], n + 1)
                dve.tensor_tensor(Pl[:, j * NQ:(j + 1) * NQ], Pf[:, j * NQ:(j + 1) * NQ],
                                  Pb[:, 2 * j * NQ + 1:2 * (j + 1) * NQ:2], ALU.subtract).then_inc(f["rest"], 1)

            dve.wait_ge(f["gexp"], 1)
            link(dve.tensor_reduce(sm(1), g(1), AX_X, ALU.add))
            link(dve.reciprocal(sm(2), sm(1)))
            link(dve.tensor_tensor(g(2), g(1), wide(sm(2)), ALU.mult))

            def first_largest(probs, largest, key_max, picked):
                link(dve.tensor_reduce(largest, probs, AX_X, ALU.max))
                link(dve.tensor_tensor(g(3), probs, wide(largest), ALU.is_equal))
                link(dve.tensor_tensor(g(4), g(3), pri[:], ALU.mult))
                link(dve.tensor_reduce(key_max, g(4), AX_X, ALU.max))
                link(dve.tensor_tensor(picked, g(4), wide(key_max), ALU.is_equal))

            first_largest(g(2), sm(3), sm(4), g(5))
            rest(0, 0)
            rest(1, 1)
            link(dve.scalar_tensor_tensor(g(6), g(5), -2.0, g(2), ALU.mult, ALU.add))
            first_largest(g(6), sm(5), sm(4), g(7))
            link(dve.tensor_tensor(sm(0), sm(3), sm(5), ALU.add))
            link(dve.tensor_scalar(sm(1), sm(0), 1e-9, None, ALU.add))
            link(dve.reciprocal(sm(2), sm(1)))
            link(dve.tensor_tensor(g(3), g(5), g(7), ALU.add))
            link(dve.tensor_tensor(g(4), g(3), g(2), ALU.mult))
            link(dve.tensor_tensor(g(0), g(4), wide(sm(2)), ALU.mult))
            dve.tensor_scalar(g(8), g(0), 1.0 / WS, None, ALU.mult).then_inc(f["gates"], 1)

            rest(2, 2)
            dve.wait_ge(f["wt_pe"], 1)
            for half in range(2):
                dve.tensor_copy(wT[:, half * 512:half * 512 + 512], psX[0:E, 2 + half, :]).then_inc(f["wt_c"], 1)
            rest(3, 3)
            dve.wait_ge(f["b2_pe"], 1)
            for half in range(2):
                yh = y[:, half * 4:half * 4 + 4, :].rearrange("p b d -> p (b d)")
                last = dve.tensor_tensor(yh, psX[:, 2 + half, :], yh, ALU.add)
            last.then_inc(f["y_dve"], 1)

            def add(e, par):
                dve.wait_ge(f["mix"], e * HT + HT)
                dve.wait_ge(f["y_dve"], e + 1)
                for b in range(QB):
                    last = dve.scalar_tensor_tensor(y[:, b, :], psX[:, 2 * par + b // 4, (b % 4) * P:(b % 4 + 1) * P],
                                                    gates[:, 8, b, ds(e, 1)], y[:, b, :], ALU.mult, ALU.add)
                last.then_inc(f["y_dve"], 1)

            for n in range(HT, HT + 1):
                rest(n, n % HT)
            add(0, 0)
            for n in range(HT + 1, 2 * HT + 1):
                rest(n, n % HT)
            add(1, 1)
            with dve.Fori(1, E // 2 - 1) as i:
                for par in range(2):
                    for j in range(HT):
                        rest(i * 2 * HT + (par * HT + j + 1), (j + 1) % HT)
                    add(i * 2 + par, par)
            for n in range((E - 2) * HT + 1, (E - 1) * HT + 1):
                rest(n, n % HT)
            add(E - 2, 0)
            for n in range((E - 1) * HT + 1, E * HT):
                rest(n, n % HT)
            add(E - 1, 1)


def newton(dve, link, root, tmp, var):
    link(dve.reciprocal(root, root))
    link(dve.tensor_tensor(tmp, root, root, ALU.mult))
    link(dve.scalar_tensor_tensor(tmp, var, EPS, tmp, ALU.add, ALU.mult))
    link(dve.tensor_scalar(tmp, tmp, -0.5, 1.5, ALU.mult, ALU.add))
    link(dve.tensor_tensor(root, root, tmp, ALU.mult))


_INS = ["x", "ctx_1024", "cond_1024", "L0_xcond_ln1_w", "L0_xcond_ln1_b", "L0_xcond_ln2_w", "L0_xcond_ln2_b",
        "L0_xcond_Wq", "L0_xcond_Wkv", "L0_xcond_Wo", "L0_ffn_gate_w", "L0_ffn_w1", "L0_ffn_b1", "L0_ffn_w2",
        "L0_ffn_b2"]
_OUTS = [((1, NQ, D), "float32")]


def kernel(**inputs):
    import numpy as _np
    import concourse.bacc as _bacc
    from concourse import mybir as _mybir
    from concourse.bass_utils import run_bass_kernel_spmd as _run

    nc = _bacc.Bacc("TRN2", target_bir_lowering=False, num_devices=1)
    arrays, args = {}, []
    for name in _INS:
        a = _np.ascontiguousarray(inputs[name])
        arrays[f"in_{name}_dram"] = a
        args.append(nc.dram_tensor(f"in_{name}_dram", a.shape, _mybir.dt.from_np(a.dtype), kind="ExternalInput").ap())
    for i, (shape, dtype) in enumerate(_OUTS):
        args.append(nc.dram_tensor(f"out_{i}_dram", shape, _mybir.dt.from_np(_np.dtype(dtype)), kind="ExternalOutput").ap())
    pixart_block(nc, *args)
    r = _run(nc, [arrays], core_ids=[0])
    return r.results[0]["out_0_dram"]
```
